# Optimizing a Trainium2 kernel written in Bass

```python
import numpy as np
import jax
import jax.numpy as jnp

def _softmax(x, axis=-1):
    return jax.nn.softmax(x, axis=axis)

def _gelu(x):
    return jax.nn.gelu(x, approximate=True)

def _silu(x):
    return jax.nn.silu(x)

def _sigmoid(x):
    return jax.nn.sigmoid(x)

def _layernorm(x, axis=-1, eps=1e-05):
    m = jnp.mean(x, axis=axis, keepdims=True)
    v = jnp.var(x, axis=axis, keepdims=True)
    return (x - m) / jnp.sqrt(v + eps)

def _scatter_add(tgt, idx, src, axis=0):
    return tgt.at[idx].add(src)

def _segment_sum(src, seg, n):
    return jax.ops.segment_sum(src, seg, n)
kernel_name = 'mk_gnn_preln_d1_gnn_r8_0395eb'

def setup_inputs(seed: int=0):
    np.random.seed(seed)
    _w = jnp.asarray

    def _rec_inputs():
        import jax
        import jax.numpy as jnp
        _gk = jax.random.key(seed)
        x = -0.000202 + 1 * jax.random.normal(jax.random.fold_in(_gk, 1), (12500, 64), jnp.float32)
        src = jax.random.randint(jax.random.fold_in(_gk, 2), (400000,), 0, 12500, jnp.int32)
        dst = jax.random.randint(jax.random.fold_in(_gk, 3), (400000,), 0, 12500, jnp.int32)
        _o = jnp.argsort(dst, stable=True)
        src = src[_o]
        dst = dst[_o]
        edge_attr_64 = -5.16925e-05 + 1.00005 * jax.random.normal(jax.random.fold_in(_gk, 12), (400000, 64), jnp.float32)
        return (x, src, dst, edge_attr_64)
    x, src, dst, edge_attr_64 = _rec_inputs()

    def _L0_gnn_setup():
        import jax, jax.numpy as jnp
        import numpy as np
        N_NODES = 12500
        N_EDGES = 200000
        N_GRAPHS = 256
        NODE = 64
        EDGE = 64
        GLOB = 64
        HID = 64

        def _lin_init(key, fan_in, fan_out):
            kw, kb = jax.random.split(key)
            bound = 1.0 / np.sqrt(fan_in)
            W = jax.random.uniform(kw, (fan_in, fan_out), minval=-bound, maxval=bound, dtype=jnp.float32)
            b = jax.random.uniform(kb, (fan_out,), minval=-bound, maxval=bound, dtype=jnp.float32)
            return (W, b)
        key = jax.random.key(seed)
        ks = jax.random.split(key, 9)
        x = jax.random.normal(ks[0], (N_NODES, NODE), dtype=jnp.float32)
        edge_index = jax.random.randint(ks[1], (2, N_EDGES), 0, N_NODES, dtype=jnp.int32)
        edge_attr = jax.random.normal(ks[2], (N_EDGES, EDGE), dtype=jnp.float32)
        u = jax.random.normal(ks[3], (N_GRAPHS, GLOB), dtype=jnp.float32)
        batch = jnp.sort(jax.random.randint(ks[4], (N_NODES,), 0, N_GRAPHS, dtype=jnp.int32))
        W1a, b1a = _lin_init(ks[5], NODE + EDGE, HID)
        W1b, b1b = _lin_init(ks[6], HID, HID)
        W2a, b2a = _lin_init(ks[7], NODE + HID + GLOB, HID)
        W2b, b2b = _lin_init(ks[8], HID, NODE)
        return {'x': x, 'edge_index': edge_index, 'edge_attr': edge_attr, 'u': u, 'batch': batch, 'W1a': W1a, 'b1a': b1a, 'W1b': W1b, 'b1b': b1b, 'W2a': W2a, 'b2a': b2a, 'W2b': W2b, 'b2b': b2b}
    _L0_gnn_all = _L0_gnn_setup()
    _L0_gnn_in = {k: v for k, v in _L0_gnn_all.items() if k in ('u', 'W1a', 'b1a', 'W1b', 'b1b', 'W2a', 'b2a', 'W2b', 'b2b')}
    del _L0_gnn_all
    return {'x': x, 'src': src, 'dst': dst, 'edge_attr_64': edge_attr_64, 'L0_gnn_u': _L0_gnn_in['u'], 'L0_gnn_W1a': _L0_gnn_in['W1a'], 'L0_gnn_b1a': _L0_gnn_in['b1a'], 'L0_gnn_W1b': _L0_gnn_in['W1b'], 'L0_gnn_b1b': _L0_gnn_in['b1b'], 'L0_gnn_W2a': _L0_gnn_in['W2a'], 'L0_gnn_b2a': _L0_gnn_in['b2a'], 'L0_gnn_W2b': _L0_gnn_in['W2b'], 'L0_gnn_b2b': _L0_gnn_in['b2b']}

def reference(x, src, dst, edge_attr_64, L0_gnn_u, L0_gnn_W1a, L0_gnn_b1a, L0_gnn_W1b, L0_gnn_b1b, L0_gnn_W2a, L0_gnn_b2a, L0_gnn_W2b, L0_gnn_b2b):
    import jax
    import jax.numpy as jnp

    def _L0_gnn_ref(x, edge_index, edge_attr, u, batch, W1a, b1a, W1b, b1b, W2a, b2a, W2b, b2b):
        import jax, jax.numpy as jnp
        import numpy as np
        N_NODES = 12500
        N_EDGES = 200000
        N_GRAPHS = 256
        NODE = 64
        EDGE = 64
        GLOB = 64
        HID = 64

        def _lin_init(key, fan_in, fan_out):
            kw, kb = jax.random.split(key)
            bound = 1.0 / np.sqrt(fan_in)
            W = jax.random.uniform(kw, (fan_in, fan_out), minval=-bound, maxval=bound, dtype=jnp.float32)
            b = jax.random.uniform(kb, (fan_out,), minval=-bound, maxval=bound, dtype=jnp.float32)
            return (W, b)
        row, col = (edge_index[0], edge_index[1])
        out = jnp.concatenate([x[row], edge_attr], axis=1)
        out = jax.nn.selu(out @ W1a + b1a) @ W1b + b1b
        summed = jax.ops.segment_sum(out, col, num_segments=x.shape[0])
        counts = jax.ops.segment_sum(jnp.ones((out.shape[0],), out.dtype), col, num_segments=x.shape[0])
        mean = summed / jnp.maximum(counts, 1.0)[:, None]
        h = jnp.concatenate([x, mean, u[batch]], axis=1)
        return jax.nn.selu(h @ W2a + b2a) @ W2b + b2b
    edge_index = jnp.stack([src, dst])
    batch0 = jnp.zeros((12500,), jnp.int32)
    h = jnp.maximum(_layernorm(x, axis=-1), 0.0)
    x = x + _L0_gnn_ref(h, edge_index, edge_attr_64, L0_gnn_u, batch0, L0_gnn_W1a, L0_gnn_b1a, L0_gnn_W1b, L0_gnn_b1b, L0_gnn_W2a, L0_gnn_b2a, L0_gnn_W2b, L0_gnn_b2b)
    return x

_drawn_inputs = setup_inputs


def setup_inputs(seed=0):
    import zlib

    import numpy as np

    out = dict(_drawn_inputs(seed))
    spreads = {}
    factors = {'edge_attr_64': 5.505, 'L0_gnn_b1a': 8.0, 'L0_gnn_b1b': 4.402}
    for name, (base, spread) in spreads.items():
        noise = np.random.default_rng([zlib.crc32(name.encode()), seed]).standard_normal(out[name].shape)
        drawn = base * np.exp(spread * noise) if base else spread * noise
        out[name] = jnp.asarray(drawn.astype(out[name].dtype))
    for name, factor in factors.items():
        out[name] = (out[name] * factor).astype(out[name].dtype)
    return out
```

```python
from contextlib import ExitStack

import numpy as np
import concourse.bass as bass
from concourse import mybir
from concourse.alu_op_type import AluOpType as ALU

F32 = mybir.dt.float32
I32 = mybir.dt.int32
ACT = mybir.ActivationFunctionType
AX = mybir.AxisListType

ALPHA = 1.6732632423543772
LAM = 1.0507009873554805
EPS = 1e-5

D = 64
NODES = 12500
NP, NT = 125, 100
EDGES = 400000
TILE = 128
TILES = EDGES // TILE
GT = 5
CG = 5
CHUNK_TILES = GT * CG
CHUNKS = TILES // CHUNK_TILES
GROUPS = TILES // GT
CE = CHUNK_TILES * TILE
WIN = 32
WIDE = 512
WIDES = -(-NODES // WIDE)
ACC_COLS = WIDES * WIDE
BANK = 512
LT = 20
LCHUNKS = NT // LT
QT = 4
QUADS = LT // QT
FT = 10
FCHUNKS = NT // FT


def build(nc, x, src_t, dst_t, dst_first, edge_t, u0, W1a, b1a, W1bT, b1b, W2a, b2a, W2b, b2b, out):
    P_dram = nc.dram_tensor("message_table", (NODES, D), F32, kind="Internal").ap()

    with ExitStack() as ctx:
        def sb(name, shape, dt=F32):
            return ctx.enter_context(nc.sbuf_tensor(name, shape, dt))

        def sem(name):
            return ctx.enter_context(nc.semaphore(name))

        x_sb = sb("x_sb", [NP, NT, D])
        Y = sb("Y", [NP, NT, D])
        acc = sb("acc", [128, ACC_COLS])
        dstl = sb("dstl", [128, TILES])
        base_i = sb("base_i", [128, GROUPS], I32)
        ea = [sb(f"ea{b}", [128, CE]) for b in range(2)]
        idx = [sb(f"idx{b}", [128, CHUNK_TILES], I32) for b in range(2)]
        G = sb("G", [128, CG, GT * D])
        E = sb("E", [128, 2, GT * D])
        S = sb("S", [128, CG, GT, D + 1])
        hot = sb("hot", [128, CG, GT, WIN])
        iota_i = sb("iota_i", [128, WIDE], I32)
        iota = sb("iota", [128, WIDE])
        ident = sb("ident", [128, 128])
        ln_alpha = sb("ln_alpha", [128, 1])
        eps = sb("eps", [128, 1])
        ones = sb("ones", [128, 128])
        inside = sb("inside", [128, 1])
        flag = sb("flag", [1, 1], I32)
        kv = sb("kv", [128, 1])
        stat = sb("stat", [NP, 4, LT])
        W_node = sb("W_node", [D + 1, 2 * D])
        W_edge = sb("W_edge", [D, D])
        W_mean = sb("W_mean", [D + 1, D + 1])
        W_out2 = sb("W_out2", [128, 128])
        W_obias = sb("W_obias", [D + 1, D])
        W2m = sb("W2m", [D, D])
        W2g = sb("W2g", [D, D])
        W1bT_s = sb("W1bT_s", [D, D])
        b1b_s = sb("b1b_s", [D, 1])
        L_mean = sb("L_mean", [D, D + 1])
        L_u0 = sb("L_u0", [D, D + 1])
        rs = sb("rs", [D, 2])
        rc = sb("rc", [NP, 2, FT])

        o = 0

        def scratch(p, n):
            nonlocal o
            o += n
            return acc[0:p, o - n:o]

        h_buf = [scratch(NP, LT * D).rearrange("p (t d) -> p t d", d=D) for _ in range(2)]
        sq = [scratch(NP, LT * D).rearrange("p (t d) -> p t d", d=D) for _ in range(2)]
        P_st = [scratch(NP, LT * D).rearrange("p (t d) -> p t d", d=D) for _ in range(2)]
        hT = [scratch(D + 1, QT * NP) for _ in range(2)]
        in_mask = scratch(128, TILES)
        assert o <= ACC_COLS
        y1 = [ea[0][0:NP, b * FT * D:(b + 1) * FT * D] for b in range(2)]
        y_exp = [ea[0][0:NP, (2 + b) * FT * D:(3 + b) * FT * D] for b in range(2)]
        vT = [ea[1][:, b * FT // 2 * NP:(b + 1) * FT // 2 * NP] for b in range(2)]
        o_st = [ea[1][0:NP, 1300 + b * FT * D:1300 + (b + 1) * FT * D] for b in range(2)]
        hot_wide = ea[1][:, 0:WIDE]

        ps = ctx.enter_context(nc.psum_tensor("ps", [128, 8, BANK], F32))

        def z_ps(q):
            return ps[:, q, 0:GT * D]

        def agg_ps(par):
            return ps[0:D + 1, 5 + par, 0:WIN]
        u_ps = ps[0:D + 1, 7, 0:D]
        wm_ps = ps[0:D + 1, 7, D:2 * D]
        ob_ps = ps[0:NP, 7, 2 * D:3 * D]
        in_ps = ps[0:1, 7, 3 * D:3 * D + 1]

        x_in = [sem(f"x_in{k}") for k in range(LCHUNKS)]
        w_in = sem("w_in")
        dst_in = sem("dst_in")
        iota_ok = sem("iota_ok")
        ident_ok = sem("ident_ok")
        clear_ok = sem("clear_ok")
        dve_self = sem("dve_self")
        slow_self = sem("slow_self")
        xc_ok = sem("xc_ok")
        sq_ok = sem("sq_ok")
        var_ok = sem("var_ok")
        std_ok = sem("std_ok")
        h_ok = sem("h_ok")
        hT_ps_ok = sem("hT_ps_ok")
        hT_ok = sem("hT_ok")
        py_ok = sem("py_ok")
        p_copied = sem("p_copied")
        y_copied = sem("y_copied")
        p_out = [sem(f"p_out{b}") for b in range(2)]
        wprep_ok = sem("wprep_ok")
        small_ok = sem("small_ok")
        mask_ok = sem("mask_ok")
        flag_ok = sem("flag_ok")
        ea_in = [sem(f"ea_in{b}") for b in range(2)]
        idx_in = [sem(f"idx_in{b}") for b in range(2)]
        g_in = [sem(f"g_in{q}") for q in range(CG)]
        z_ok = sem("z_ok")
        er_ok = sem("er_ok")
        s_ok = sem("s_ok")
        hot_ok = sem("hot_ok")
        agg_ok = sem("agg_ok")
        acc_ok = sem("acc_ok")
        slot_taken = sem("slot_taken")
        slow_step = sem("slow_step")
        slow_tile = sem("slow_tile")
        slow_ea = sem("slow_ea")
        slow_idx = sem("slow_idx")
        slow_g = sem("slow_g")
        slow_z = sem("slow_z")
        slow_er = sem("slow_er")
        slow_s = sem("slow_s")
        slow_hot = sem("slow_hot")
        slow_agg = sem("slow_agg")
        slow_acc = sem("slow_acc")
        totals_ok = sem("totals_ok")
        zm_ok = sem("zm_ok")
        y1_ok = sem("y1_ok")
        yer_ok = sem("yer_ok")
        v_ok = sem("v_ok")
        vT_ps_ok = sem("vT_ps_ok")
        vT_ok = sem("vT_ok")
        o_ps_ok = sem("o_ps_ok")
        o_ok = sem("o_ok")
        o_out = [sem(f"o_out{b}") for b in range(2)]

        x_v = x.rearrange("(p t) d -> p t d", t=NT)
        P_v = P_dram.rearrange("(p t) d -> p t d", t=NT)
        out_v = out.rearrange("(p t) d -> p t d", t=NT)
        N_W = 15 * 16

        block = ctx.enter_context(nc.Block())

        @block.sync
        def _(sp):
            sp.dma_start(base_i[:, :], dst_first.broadcast_to((128, GROUPS))).then_inc(dst_in, 16)
            sp.dma_start(dstl[:, :].bitcast(I32), dst_t).then_inc(dst_in, 16)

            def load_chunk(c, par):
                sp.dma_start(idx[par][:, :], src_t[:, bass.ds(c * CHUNK_TILES, CHUNK_TILES)]).then_inc(idx_in[par], 16)
                sp.dma_start(ea[par][0:D, :], edge_t[bass.ds(c, 1), :, :].rearrange("c d e -> (c d) e")).then_inc(ea_in[par], 16)

            load_chunk(0, 0)
            load_chunk(1, 1)
            with sp.Fori(0, (CHUNKS - 3) // 2) as i:
                for k in range(2):
                    sp.wait_ge(z_ok, (i * 2 + (k + 1)) * CG)
                    load_chunk(i * 2 + (k + 2), k)
            sp.wait_ge(z_ok, (CHUNKS - 2) * CG)
            load_chunk(CHUNKS - 1, 0)

            sp.wait_ge(flag_ok, 1)
            with sp.If(sp.value_load(flag[0:1, 0:1], min_val=0, max_val=EDGES) != 0):
                with sp.Fori(0, CHUNKS) as c:
                    with sp.Fori(0, CHUNK_TILES) as k:
                        t = c * CHUNK_TILES + k
                        sp.wait_ge(slow_tile, t + 1)
                        sp.sem_inc(slow_step, 1)
                        sp.dma_start(idx[0][:, 0:1], src_t[:, bass.ds(t, 1)], allow_slow_non_contiguous=True).then_inc(slow_idx, 16)
                        sp.dma_start(ea[0][0:D, 0:TILE],
                                     edge_t[bass.ds(c, 1), :, bass.ds(k * TILE, TILE)].rearrange("c d e -> (c d) e")
                                     ).then_inc(slow_ea, 16)

        @block.gpsimd
        def _(pool):
            for k in range(LCHUNKS):
                pool.dma_start(x_sb[:, k * LT:(k + 1) * LT, :], x_v[:, k * LT:(k + 1) * LT, :]).then_inc(x_in[k], 16)
            nc.gpsimd.memset(ident[:, :], 0.0).then_inc(ident_ok, 1)
            pool.wait_ge(ident_ok, 1)
            nc.gpsimd.affine_select(out=ident[:, :], in_=ident[:, :], compare_op=ALU.not_equal, fill=1.0, base=0,
                                    pattern=[[-1, 128]], channel_multiplier=1).then_inc(ident_ok, 1)
            nc.gpsimd.iota(iota_i[:, :], [[1, WIDE]], base=0, channel_multiplier=0).then_inc(iota_ok, 1)
            for k in range(LCHUNKS):
                pool.wait_ge(p_copied, QUADS * (k + 1))
                pool.dma_start(P_v[:, k * LT:(k + 1) * LT, :], P_st[k % 2]).then_inc(p_out[k % 2], 16)
            pool.wait_ge(p_out[0], 16 * ((LCHUNKS + 1) // 2))
            pool.wait_ge(p_out[1], 16 * (LCHUNKS // 2))

            def gather_chunk(c, par, n, first=False):
                pool.wait_ge(idx_in[par], (n + 1) * 16)
                pool.sem_inc(slot_taken, 1)
                for q in range(CG):
                    if not first:
                        pool.wait_ge(z_ok, c * CG + (q + 1 - CG))
                        pool.sem_inc(slot_taken, 1)
                    for t in range(GT):
                        pool.indirect_dma_start(G[:, q, t * D:(t + 1) * D], None, P_dram,
                                                bass.IndirectOffsetOnAxis(idx[par][:, q * GT + t:q * GT + t + 1], 0)
                                                ).then_inc(g_in[q], 16)

            gather_chunk(0, 0, 0, first=True)
            with pool.Fori(0, (CHUNKS - 1) // 2) as i:
                gather_chunk(i * 2 + 1, 1, i)
                gather_chunk(i * 2 + 2, 0, i + 1)

            pool.wait_ge(flag_ok, 1)
            with pool.If(pool.value_load(flag[0:1, 0:1], min_val=0, max_val=EDGES) != 0):
                with pool.Fori(0, TILES) as t:
                    pool.wait_ge(slow_tile, t + 1)
                    pool.wait_ge(slow_idx, (t + 1) * 16)
                    pool.sem_inc(slow_step, 1)
                    pool.indirect_dma_start(G[:, 0, 0:D], None, P_dram,
                                            bass.IndirectOffsetOnAxis(idx[0][:, 0:1], 0)).then_inc(slow_g, 16)

            for k in range(FCHUNKS):
                pool.wait_ge(o_ok, k + 1)
                pool.dma_start(out_v[:, k * FT:(k + 1) * FT, :],
                               o_st[k % 2].rearrange("p (t d) -> p t d", d=D)).then_inc(o_out[k % 2], 16)
            for b in range(2):
                pool.wait_ge(o_out[b], 16 * (FCHUNKS // 2))

        @block.scalar
        def _(act):
            act.wait_ge(clear_ok, 1)
            for dst_ap, src_ap in (
                (W_node[0:D, 0:D], W1a[0:D, :]), (W_node[0:D, D:2 * D], W2a[0:D, :]),
                (W_node[D:D + 1, 0:D], b1a), (W_node[D:D + 1, D:2 * D], b2a),
                (L_u0[:, D:D + 1], u0), (W2g[:, :], W2a[2 * D:3 * D, :]),
                (W_edge[:, :], W1a[D:2 * D, :]), (W2m[:, :], W2a[D:2 * D, :]),
                (W1bT_s[:, :], W1bT), (b1b_s[:, :], b1b),
                (W_out2[0:D, 0:D], W2b), (W_out2[D:2 * D, D:2 * D], W2b),
                (W_obias[0:D, :], W2b), (W_obias[D:D + 1, :], b2b), (rs[:, 1:2], b1b),
            ):
                act.dma_start(dst_ap, src_ap).then_inc(w_in, 16)

            def copy_y(n):
                act.wait_ge(py_ok, n + 1)
                nc.scalar.copy(Y[:, n * QT:(n + 1) * QT, :],
                               ps[0:NP, 4 + n % 2, 0:QT * D].rearrange("p (t d) -> p t d", d=D)
                               ).then_inc(y_copied, 1)

            def square(k):
                act.wait_ge(xc_ok, k + 1)
                if k >= 2:
                    act.wait_ge(var_ok, k - 1)
                nc.scalar.activation(sq[k % 2], h_buf[k % 2], ACT.Square).then_inc(sq_ok, 1)
                act.wait_ge(var_ok, k + 1)
                nc.scalar.activation(stat[:, 2, :], stat[:, 1, :], ACT.Sqrt, bias=eps[0:NP, :],
                                     scale=1.0 / D).then_inc(std_ok, 1)

            square(0)
            for k in range(LCHUNKS):
                if k + 1 < LCHUNKS:
                    square(k + 1)
                for r in range(QUADS):
                    n = k * QUADS + r
                    act.wait_ge(hT_ps_ok, n + 1)
                    if n >= 2:
                        act.wait_ge(py_ok, n - 1)
                    nc.scalar.copy(hT[n % 2][0:D, :], ps[0:D, n % 2, 0:QT * NP]).then_inc(hT_ok, 1)
                    if n >= 1:
                        copy_y(n - 1)
            copy_y(LCHUNKS * QUADS - 1)

            def exp_relu(c, par, q, first=False):
                act.wait_ge(z_ok, c * CG + (q + 1))
                if not (first and q < 2):
                    act.wait_ge(s_ok, c * CG + (q - 1))
                nc.scalar.activation(E[:, (par + q) % 2, :], z_ps(q), ACT.Exp, bias=ln_alpha[:, :])
                nc.scalar.activation(z_ps(q), z_ps(q), ACT.Relu).then_inc(er_ok, 1)

            for q in range(CG):
                exp_relu(0, 0, q, first=True)
            with act.Fori(0, (CHUNKS - 1) // 2) as i:
                for q in range(CG):
                    exp_relu(i * 2 + 1, 1, q)
                for q in range(CG):
                    exp_relu(i * 2 + 2, 0, q)

            act.wait_ge(flag_ok, 1)
            with act.If(act.value_load(flag[0:1, 0:1], min_val=0, max_val=EDGES) != 0):
                with act.Fori(0, TILES) as t:
                    act.wait_ge(slow_z, t + 1)
                    nc.scalar.activation(E[:, 0, 0:D], ps[:, 0, 0:D], ACT.Exp, bias=ln_alpha[:, :])
                    nc.scalar.activation(ps[:, 0, 0:D], ps[:, 0, 0:D], ACT.Relu).then_inc(slow_er, 1)

            def transposed(k):
                act.wait_ge(vT_ps_ok, k + 1)
                if k >= 2:
                    act.wait_ge(o_ps_ok, k - 1)
                nc.scalar.copy(vT[k % 2][:, 0:3 * NP], ps[:, 4, 0:3 * NP])
                nc.scalar.copy(vT[k % 2][:, 3 * NP:5 * NP], ps[:, 5, 0:2 * NP]).then_inc(vT_ok, 1)

            for k in range(FCHUNKS):
                act.wait_ge(y1_ok, k + 1)
                if k >= 2:
                    act.wait_ge(v_ok, k - 1)
                nc.scalar.activation(y_exp[k % 2], y1[k % 2], ACT.Exp, bias=ln_alpha[0:NP, :])
                nc.scalar.activation(y1[k % 2], y1[k % 2], ACT.Relu).then_inc(yer_ok, 1)
                if k >= 1:
                    transposed(k - 1)
            transposed(FCHUNKS - 1)

        @block.vector
        def _(dve):
            steps = {dve_self: 0, slow_self: 0}

            def link(ins, s=dve_self):
                steps[s] += 1
                ins.then_inc(s, 1)
                dve.wait_ge(s, steps[s])

            nc.vector.memset(W_out2[:, :], 0.0)
            nc.vector.memset(L_u0[:, :], 0.0)
            nc.vector.memset(W_mean[:, :], 0.0)
            nc.vector.memset(ln_alpha[:, :], float(np.log(ALPHA)))
            nc.vector.memset(eps[:, :], EPS)
            nc.vector.memset(ones[:, :], 1.0)
            for b in range(2):
                nc.vector.memset(hT[b][D:D + 1, :], 1.0)
            link(nc.vector.memset(S[:, :, :, D:D + 1], 1.0))
            nc.vector.memset(W_mean[D:D + 1, D:D + 1], 1.0).then_inc(clear_ok, 1)

            def normalise(k):
                dve.wait_ge(x_in[k], 16)
                xk = x_sb[:, k * LT:(k + 1) * LT, :]
                h = h_buf[k % 2]
                link(nc.vector.tensor_reduce(out=stat[:, 0, :], in_=xk, op=ALU.add, axis=AX.X))
                link(nc.vector.tensor_scalar(stat[:, 3, :], stat[:, 0, :], -1.0 / D, None, ALU.mult))
                if k >= 2:
                    dve.wait_ge(hT_ps_ok, QUADS * (k - 1))
                nc.vector.tensor_tensor(h, xk, stat[:, 3, :].rearrange("p (t o) -> p t o", o=1).broadcast_to((NP, LT, D)),
                                        ALU.add).then_inc(xc_ok, 1)
                dve.wait_ge(sq_ok, k + 1)
                nc.vector.tensor_reduce(out=stat[:, 1, :], in_=sq[k % 2], op=ALU.add, axis=AX.X).then_inc(var_ok, 1)
                dve.wait_ge(std_ok, k + 1)
                link(nc.vector.reciprocal(stat[:, 3, :], stat[:, 2, :]))
                nc.vector.scalar_tensor_tensor(
                    out=h, in0=h, scalar=0.0, in1=stat[:, 3, :].rearrange("p (t o) -> p t o", o=1).broadcast_to((NP, LT, D)),
                    op0=ALU.max, op1=ALU.mult).then_inc(h_ok, 1)

            def prepare_weights():
                dve.wait_ge(w_in, N_W)
                link(nc.vector.tensor_reduce(out=rs[:, 0:1], in_=W1bT_s[:, :], op=ALU.add, axis=AX.X))
                nc.vector.scalar_tensor_tensor(out=L_mean[:, D:D + 1], in0=rs[:, 0:1], scalar=-ALPHA * LAM, in1=b1b_s[:, :],
                                               op0=ALU.mult, op1=ALU.add)
                nc.vector.tensor_scalar(L_mean[:, 0:D], W1bT_s[:, :], LAM, None, ALU.mult)
                nc.vector.tensor_scalar(W_obias[0:D, :], W_obias[0:D, :], -ALPHA * LAM, None, ALU.mult)
                link(nc.vector.tensor_scalar(W_out2[:, :], W_out2[:, :], LAM, None, ALU.mult))
                nc.vector.tensor_copy(iota[:, 0:1], eps[:, :]).then_inc(wprep_ok, 1)
                dve.wait_ge(small_ok, 3)
                nc.vector.tensor_copy(W_mean[:, 0:D], wm_ps)
                nc.vector.tensor_tensor(W_node[D:D + 1, D:2 * D], W_node[D:D + 1, D:2 * D], u_ps[D:D + 1, :],
                                        ALU.add).then_inc(wprep_ok, 1)

            prepare_weights()
            normalise(0)
            for k in range(LCHUNKS):
                if k + 1 < LCHUNKS:
                    normalise(k + 1)
                for r in range(QUADS):
                    n = k * QUADS + r
                    dve.wait_ge(py_ok, n + 1)
                    if k >= 2 and r == 0:
                        dve.wait_ge(p_out[k % 2], 16 * (k // 2))
                    nc.vector.tensor_copy(P_st[k % 2][:, r * QT:(r + 1) * QT, :],
                                          ps[0:NP, 2 + n % 2, 0:QT * D].rearrange("p (t d) -> p t d", d=D)
                                          ).then_inc(p_copied, 1)

            dve.wait_ge(iota_ok, 1)
            nc.vector.tensor_copy(iota[:, :], iota_i[:, :])
            dve.wait_ge(dst_in, 32)
            link(nc.vector.tensor_tensor(
                dstl[:, :].rearrange("p (g t) -> p g t", t=GT), dstl[:, :].bitcast(I32).rearrange("p (g t) -> p g t", t=GT),
                base_i[:, :].rearrange("p (g o) -> p g o", o=1).broadcast_to((128, GROUPS, GT)), ALU.subtract))

            def mask_inside():
                link(nc.vector.tensor_scalar(in_mask, dstl[:, :], 0.0, None, ALU.is_ge))
                link(nc.vector.scalar_tensor_tensor(out=in_mask, in0=dstl[:, :], scalar=float(WIN), in1=in_mask,
                                                    op0=ALU.is_lt, op1=ALU.mult))

            mask_inside()
            nc.vector.tensor_reduce(out=inside[:, :], in_=in_mask, op=ALU.add, axis=AX.X).then_inc(mask_ok, 1)
            dve.wait_ge(small_ok, 4)
            nc.vector.tensor_scalar(flag[:, :], in_ps, -1.0, float(EDGES), ALU.mult, ALU.add).then_inc(flag_ok, 1)
            dve.wait_ge(y_copied, LCHUNKS * QUADS)
            dve.wait_ge(p_out[0], 16 * ((LCHUNKS + 1) // 2))
            dve.wait_ge(p_out[1], 16 * (LCHUNKS // 2))
            link(nc.vector.memset(acc[:, :], 0.0))
            link(nc.vector.tensor_tensor(
                x_sb[:, :, :], x_sb[:, :, :], ob_ps.rearrange("p (o d) -> p o d", o=1).broadcast_to((NP, NT, D)), ALU.add))

            def add_window(g, bank):
                base = dve.value_load(base_i[0:1, bass.ds(g, 1)], min_val=0, max_val=NODES - 1)
                dve.wait_ge(agg_ok, g + 1)
                window = acc[0:D + 1, bass.ds(base, WIN)]
                nc.vector.tensor_tensor(window, window, agg_ps(bank), ALU.add).then_inc(acc_ok, 1)

            def combine(c, par, q, first=False):
                g = c * CG + q
                if not first:
                    dve.wait_ge(agg_ok, c * CG + (q + 1 - CG))
                nc.vector.tensor_tensor(
                    hot[:, q, :, :], iota[:, 0:WIN].rearrange("p (o w) -> p o w", o=1).broadcast_to((128, GT, WIN)),
                    dstl[:, bass.ds(c * CHUNK_TILES + q * GT, GT)].rearrange("p (t o) -> p t o", o=1).broadcast_to(
                        (128, GT, WIN)), ALU.is_equal).then_inc(hot_ok, 1)
                dve.wait_ge(er_ok, c * CG + (q + 1))
                nc.vector.scalar_tensor_tensor(
                    out=S[:, q, :, 0:D], in0=E[:, (par + q) % 2, :].rearrange("p (t d) -> p t d", d=D), scalar=ALPHA,
                    in1=z_ps(q).rearrange("p (t d) -> p t d", d=D), op0=ALU.min, op1=ALU.add).then_inc(s_ok, 1)
                if not (first and q == 0):
                    if not (first and q == 1):
                        dve.wait_ge(acc_ok, c * CG + (q - 1))
                    add_window(c * CG + (q - 1), (par + q + 1) % 2)

            for q in range(CG):
                combine(0, 0, q, first=True)
            with dve.Fori(0, (CHUNKS - 1) // 2) as i:
                for q in range(CG):
                    combine(i * 2 + 1, 1, q)
                for q in range(CG):
                    combine(i * 2 + 2, 0, q)
            dve.wait_ge(acc_ok, GROUPS - 1)
            add_window(GROUPS - 1, (GROUPS - 1) % 2)
            dve.wait_ge(acc_ok, GROUPS)

            with dve.If(dve.value_load(flag[0:1, 0:1], min_val=0, max_val=EDGES) != 0):
                mask = ea[0][:, 0:TILES]
                base_b = base_i[:, :].rearrange("p (g o) -> p g o", o=1).broadcast_to((128, GROUPS, GT))
                as_groups = lambda a: a.rearrange("p (g t) -> p g t", t=GT)
                link(nc.vector.tensor_scalar(mask, dstl[:, :], 0.0, None, ALU.is_ge), slow_self)
                link(nc.vector.scalar_tensor_tensor(out=mask, in0=dstl[:, :], scalar=float(WIN), in1=mask,
                                                    op0=ALU.is_lt, op1=ALU.mult), slow_self)
                link(nc.vector.tensor_tensor(as_groups(dstl[:, :]), as_groups(dstl[:, :]), base_b, ALU.add), slow_self)
                link(nc.vector.scalar_tensor_tensor(out=dstl[:, :], in0=mask, scalar=-2.0 * ACC_COLS, in1=dstl[:, :],
                                                    op0=ALU.mult, op1=ALU.add), slow_self)
                nc.vector.tensor_copy(kv[:, :], dstl[:, 0:1]).then_inc(slow_tile, 1)
                nc.vector.tensor_copy(kv[:, :], dstl[:, 0:1]).then_inc(slow_acc, 1)
                with dve.Fori(0, TILES) as t:
                    dve.wait_ge(slow_er, t + 1)
                    nc.vector.scalar_tensor_tensor(out=S[:, 0, 0, 0:D], in0=E[:, 0, 0:D], scalar=ALPHA, in1=ps[:, 0, 0:D],
                                                   op0=ALU.min, op1=ALU.add).then_inc(slow_s, 1)
                    dve.wait_ge(slow_acc, t * WIDES + 1)
                    nc.vector.tensor_copy(kv[:, :], dstl[:, bass.ds(t, 1)]).then_inc(slow_s, 1)
                    dve.wait_ge(slow_s, (t + 1) * 2)
                    dve.sem_inc(slow_step, 1)
                    with dve.Fori(0, WIDES) as v:
                        n = t * WIDES + v
                        dve.wait_ge(slow_acc, n + 1)
                        nc.vector.tensor_scalar(hot_wide, iota[:, :], kv[:, 0:1], None, ALU.is_equal).then_inc(slow_hot, 1)
                        dve.wait_ge(slow_agg, n + 1)
                        nc.vector.tensor_scalar(kv[:, :], kv[:, :], -float(WIDE), None, ALU.add)
                        wide = acc[0:D + 1, bass.ds(v * WIDE, WIDE)]
                        nc.vector.tensor_tensor(wide, wide, ps[0:D + 1, 5, :], ALU.add).then_inc(slow_acc, 1)
                    dve.wait_ge(slow_acc, t * WIDES + (WIDES + 1))
                    dve.sem_inc(slow_tile, 1)

            nc.vector.tensor_copy(kv[:, :], eps[:, :]).then_inc(totals_ok, 1)

            def first_layer(k):
                dve.wait_ge(zm_ok, k + 1)
                zm = ps[0:NP, 2 * (k % 2):2 * (k % 2) + 2, 0:5 * (D + 1)].rearrange("p b (t d) -> p b t d", d=D + 1)
                as_bt = lambda a: a.rearrange("p (b t) -> p b t", b=2)
                link(nc.vector.tensor_scalar(as_bt(rc[:, 0, :]).rearrange("p b (t o) -> p b t o", o=1), zm[:, :, :, D:D + 1], 1.0, None, ALU.max))
                link(nc.vector.reciprocal(rc[:, 1, :], rc[:, 0, :]))
                y = y1[k % 2].rearrange("p (b t d) -> p b t d", b=2, d=D)
                if k >= 2:
                    dve.wait_ge(vT_ps_ok, k - 1)
                link(nc.vector.tensor_tensor(
                    y, zm[:, :, :, 0:D],
                    as_bt(rc[:, 1, :]).rearrange("p b (t o) -> p b t o", o=1).broadcast_to((NP, 2, 5, D)), ALU.mult))
                nc.vector.tensor_tensor(y1[k % 2], y1[k % 2], Y[:, k * FT:(k + 1) * FT, :].rearrange("p t d -> p (t d)"),
                                        ALU.add).then_inc(y1_ok, 1)

            def output(k):
                dve.wait_ge(o_ps_ok, k + 1)
                if k >= 2:
                    dve.wait_ge(o_out[k % 2], 16 * (k // 2))
                xk = x_sb[:, k * FT:(k + 1) * FT, :].rearrange("p t d -> p (t d)")
                nc.vector.tensor_tensor(o_st[k % 2][:, 0:6 * D], ps[0:NP, 6, 0:6 * D], xk[:, 0:6 * D], ALU.add)
                nc.vector.tensor_tensor(o_st[k % 2][:, 6 * D:10 * D], ps[0:NP, 7, 0:4 * D], xk[:, 6 * D:10 * D],
                                        ALU.add).then_inc(o_ok, 1)

            for k in range(FCHUNKS):
                first_layer(k)
                dve.wait_ge(yer_ok, k + 1)
                nc.vector.scalar_tensor_tensor(out=y1[k % 2], in0=y_exp[k % 2], scalar=ALPHA, in1=y1[k % 2],
                                               op0=ALU.min, op1=ALU.add).then_inc(v_ok, 1)
                if k >= 1:
                    output(k - 1)
            output(FCHUNKS - 1)

        @block.tensor
        def _(pe):
            mm = nc.tensor.matmul
            pe.wait_ge(wprep_ok, 1)
            mm(u_ps, L_u0[:, :], W2g[:, :], start=True, stop=True).then_inc(small_ok, 1)
            mm(wm_ps, L_mean[:, :], W2m[:, :], start=True, stop=True).then_inc(small_ok, 1)
            mm(ob_ps, ones[0:D + 1, 0:NP], W_obias[:, :], start=True, stop=True).then_inc(small_ok, 1)
            pe.wait_ge(ident_ok, 2)
            pe.wait_ge(wprep_ok, 2)

            def node_products(n):
                pe.wait_ge(hT_ok, n + 1)
                if n >= 2:
                    pe.wait_ge(p_copied, n - 1)
                    pe.wait_ge(y_copied, n - 1)
                for half in range(2):
                    for t in range(QT):
                        last = mm(ps[0:NP, 2 + 2 * half + n % 2, t * D:(t + 1) * D], hT[n % 2][:, t * NP:(t + 1) * NP],
                                  W_node[:, half * D:(half + 1) * D], start=True, stop=True)
                last.then_inc(py_ok, 1)

            for n in range(LCHUNKS * QUADS):
                pe.wait_ge(h_ok, n // QUADS + 1)
                if n >= 2:
                    pe.wait_ge(hT_ok, n - 1)
                h = h_buf[(n // QUADS) % 2]
                for t in range(QT):
                    last = nc.tensor.transpose(ps[0:D, n % 2, t * NP:(t + 1) * NP], h[:, (n % QUADS) * QT + t, :],
                                               ident[0:NP, 0:NP])
                last.then_inc(hT_ps_ok, 1)
                if n >= 1:
                    node_products(n - 1)
            node_products(LCHUNKS * QUADS - 1)
            pe.wait_ge(mask_ok, 1)
            mm(in_ps, inside[:, :], ones[:, 0:1], start=True, stop=True).then_inc(small_ok, 1)
            pe.wait_ge(p_copied, LCHUNKS * QUADS)
            pe.wait_ge(y_copied, LCHUNKS * QUADS)

            def sum_group(c, par, q, first=False):
                pq = (q - 1) % CG
                pe.wait_ge(s_ok, c * CG + q)
                pe.wait_ge(hot_ok, c * CG + q)
                if not (first and q < 3):
                    pe.wait_ge(acc_ok, c * CG + (q - 2))
                for t in range(GT):
                    last = mm(agg_ps((par + q + 1) % 2), S[:, pq, t, :], hot[:, pq, t, :], start=(t == 0), stop=(t == GT - 1))
                last.then_inc(agg_ok, 1)

            def edge_group(c, par, n, q, first=False):
                if q == 0:
                    pe.wait_ge(ea_in[par], (n + 1) * 16)
                pe.wait_ge(g_in[q], (c + 1) * (16 * GT))
                if not first:
                    pe.wait_ge(s_ok, c * CG + (q + 1 - CG))
                mm(z_ps(q), ident[:, :], G[:, q, :], start=True, stop=False)
                for t in range(GT):
                    e0 = (q * GT + t) * TILE
                    last = mm(z_ps(q)[:, t * D:(t + 1) * D], ea[par][0:D, e0:e0 + TILE], W_edge[:, :],
                              start=False, stop=(t == GT - 1))
                last.then_inc(z_ok, 1)
                if not (first and q == 0):
                    sum_group(c, par, q, first)

            for q in range(CG):
                edge_group(0, 0, 0, q, first=True)
            with pe.Fori(0, (CHUNKS - 1) // 2) as i:
                for q in range(CG):
                    edge_group(i * 2 + 1, 1, i, q)
                for q in range(CG):
                    edge_group(i * 2 + 2, 0, i + 1, q)
            sum_group(CHUNKS, CHUNKS % 2, 0)

            pe.wait_ge(flag_ok, 1)
            with pe.If(pe.value_load(flag[0:1, 0:1], min_val=0, max_val=EDGES) != 0):
                with pe.Fori(0, TILES) as t:
                    pe.wait_ge(slow_g, (t + 1) * 16)
                    pe.wait_ge(slow_ea, (t + 1) * 16)
                    mm(ps[:, 0, 0:D], ident[:, :], G[:, 0, 0:D], start=True, stop=False)
                    mm(ps[:, 0, 0:D], ea[0][0:D, 0:TILE], W_edge[:, :], start=False, stop=True).then_inc(slow_z, 1)
                    pe.wait_ge(slow_s, (t + 1) * 2)
                    pe.sem_inc(slow_step, 1)
                    with pe.Fori(0, WIDES) as v:
                        pe.wait_ge(slow_hot, t * WIDES + v + 1)
                        mm(ps[0:D + 1, 5, :], S[:, 0, 0, :], hot_wide, start=True, stop=True).then_inc(slow_agg, 1)

            pe.wait_ge(totals_ok, 1)

            def mean_products(k):
                if k >= 2:
                    pe.wait_ge(y1_ok, k - 1)
                for j in range(FT):
                    t = k * FT + j
                    last = mm(ps[0:NP, 2 * (k % 2) + j // 5, (j % 5) * (D + 1):(j % 5 + 1) * (D + 1)],
                              acc[0:D + 1, t:NODES:NT], W_mean[:, :], start=True, stop=True)
                last.then_inc(zm_ok, 1)

            mean_products(0)
            for k in range(FCHUNKS):
                if k + 1 < FCHUNKS:
                    mean_products(k + 1)
                pe.wait_ge(v_ok, k + 1)
                if k >= 1:
                    pe.wait_ge(vT_ok, k)
                for j in range(FT // 2):
                    bank, col = (4, j) if j < 3 else (5, j - 3)
                    last = nc.tensor.transpose(ps[:, bank, col * NP:(col + 1) * NP], y1[k % 2][:, j * 2 * D:(j + 1) * 2 * D],
                                               ident[0:NP, 0:NP])
                last.then_inc(vT_ps_ok, 1)
                pe.wait_ge(vT_ok, k + 1)
                if k >= 1:
                    pe.wait_ge(o_ok, k)
                for j in range(FT // 2):
                    bank, col = (6, j) if j < 3 else (7, j - 3)
                    last = mm(ps[0:NP, bank, col * 2 * D:(col + 1) * 2 * D], vT[k % 2][:, j * NP:(j + 1) * NP],
                              W_out2[:, :], start=True, stop=True)
                last.then_inc(o_ps_ok, 1)


def kernel(x, src, dst, edge_attr_64, L0_gnn_u, L0_gnn_W1a, L0_gnn_b1a, L0_gnn_W1b, L0_gnn_b1b, L0_gnn_W2a, L0_gnn_b2a,
           L0_gnn_W2b, L0_gnn_b2b):
    import concourse.bacc as bacc
    from concourse.bass_utils import run_bass_kernel_spmd

    a = np.asarray
    arrays = {
        "x": a(x),
        "src_t": np.ascontiguousarray(a(src).reshape(TILES, TILE).T),
        "dst_t": np.ascontiguousarray(a(dst).reshape(TILES, TILE).T),
        "dst_first": np.ascontiguousarray(a(dst).reshape(GROUPS, GT * TILE)[:, 0].reshape(1, GROUPS)),
        "edge_t": np.ascontiguousarray(a(edge_attr_64).reshape(CHUNKS, CE, D).transpose(0, 2, 1)),
        "u0": np.ascontiguousarray(a(L0_gnn_u)[0].reshape(D, 1)),
        "W1a": a(L0_gnn_W1a),
        "b1a": a(L0_gnn_b1a).reshape(1, D),
        "W1bT": np.ascontiguousarray(a(L0_gnn_W1b).T),
        "b1b": a(L0_gnn_b1b).reshape(D, 1),
        "W2a": a(L0_gnn_W2a),
        "b2a": a(L0_gnn_b2a).reshape(1, D),
        "W2b": a(L0_gnn_W2b),
        "b2b": a(L0_gnn_b2b).reshape(1, D),
    }
    nc = bacc.Bacc("TRN2", target_bir_lowering=False, num_devices=1)
    args = [nc.dram_tensor(name, v.shape, mybir.dt.from_np(v.dtype), kind="ExternalInput").ap() for name, v in arrays.items()]
    out = nc.dram_tensor("out", (NODES, D), F32, kind="ExternalOutput").ap()
    build(nc, *args, out)
    r = run_bass_kernel_spmd(nc, [arrays], core_ids=[0])
    return r.results[0]["out"]
```

```python
from contextlib import ExitStack

import numpy as np
import concourse.bass as bass
from concourse import mybir
from concourse.alu_op_type import AluOpType as ALU

F32 = mybir.dt.float32
I32 = mybir.dt.int32
ACT = mybir.ActivationFunctionType
AX = mybir.AxisListType

ALPHA = 1.6732632423543772
LAM = 1.0507009873554805
EPS = 1e-5

D = 64
NODES = 12500
NP, NT = 125, 100
SPLIT = 112
EDGES = 400000
TILE = 128
TILES = EDGES // TILE
GT = 5
CG = 5
CHUNK_TILES = GT * CG
CHUNKS = TILES // CHUNK_TILES
GROUPS = TILES // GT
CE = CHUNK_TILES * TILE
RAW = 2
RING = 2 * CG
WIN = 32
WIDE = 512
WIDES = -(-NODES // WIDE)
ACC_COLS = WIDES * WIDE
BANK = 512
LT = 20
LCHUNKS = NT // LT
QT = 4
M = NODES // CHUNKS
assert M * CHUNKS == NODES and M <= 128


def build(nc, x, src_t, dst_t, dst_first, edge_t, u0, W1a, b1a, W1bT, b1b, W2a, b2a, W2b, b2b, out):
    P_dram = nc.dram_tensor("message_table", (NODES, D), F32, kind="Internal").ap()
    h_dram = nc.dram_tensor("normed", (NODES, D), F32, kind="Internal").ap()

    with ExitStack() as ctx:
        def sb(name, shape, dt=F32):
            return ctx.enter_context(nc.sbuf_tensor(name, shape, dt))

        def sem(name):
            return ctx.enter_context(nc.semaphore(name))

        x_sb = sb("x_sb", [128, NT * D])
        raw = sb("raw", [128, RAW * CHUNK_TILES, D])
        sq = sb("sq", [128, 2, LT, D])
        P_st = sb("P_st", [NP, 2, LT, D])
        hT = sb("hT", [128, 2, QT // 2 * 128])
        stat = sb("stat", [128, 4, LT])
        acc = sb("acc", [128, ACC_COLS])
        dstl = sb("dstl", [128, TILES])
        base_i = sb("base_i", [128, GROUPS], I32)
        due_i = sb("due_i", [128, GROUPS], I32)
        ea = [sb(f"ea{b}", [128, CE]) for b in range(2)]
        idx = [sb(f"idx{b}", [128, CHUNK_TILES], I32) for b in range(2)]
        G = sb("G", [128, RING, GT * D])
        Z = sb("Z", [128, 2, GT * D])
        E = sb("E", [128, 2, GT * D])
        S = sb("S", [128, CG, GT, D + 1])
        hot = sb("hot", [128, CG, GT, WIN])
        iota_i = sb("iota_i", [128, WIDE], I32)
        iota = sb("iota", [128, WIDE])
        ident = sb("ident", [128, 128])
        ln_alpha = sb("ln_alpha", [128, 1])
        eps = sb("eps", [128, 1])
        zero = sb("zero", [128, 1])
        one = sb("one", [128, 1])
        inside = sb("inside", [128, 1])
        late = sb("late", [128, 1])
        flag = sb("flag", [1, 2], I32)
        flag_f = sb("flag_f", [1, 1])
        kv = sb("kv", [128, 1])
        W_pair = sb("W_pair", [128, 128])
        b1a_rows = sb("b1a_rows", [128, D])
        W_edge = sb("W_edge", [D, D])
        W_h = sb("W_h", [D + 1, D])
        W_mean = sb("W_mean", [D + 1, D + 1])
        W_out = sb("W_out", [D + 1, D])
        W2m = sb("W2m", [D, D])
        W2g = sb("W2g", [D, D])
        W2b_s = sb("W2b_s", [D, D])
        W1bT_s = sb("W1bT_s", [D, D])
        b1b_s = sb("b1b_s", [D, 1])
        L_mean = sb("L_mean", [D, D + 1])
        L_u0 = sb("L_u0", [D, D + 1])
        L_one = sb("L_one", [D, D + 1])
        rs = sb("rs", [D, 1])
        hx = sb("hx", [M, 2, 2, D])
        nhT = sb("nhT", [D + 1, M])
        tot = sb("tot", [D + 1, M])
        rc = sb("rc", [M, 2])
        y = sb("y", [M, D])
        y_exp = sb("y_exp", [M, D])
        nvT = sb("nvT", [D + 1, M])
        o_st = sb("o_st", [M, 2, D])
        hot_wide = ea[1][:, 0:WIDE]
        in_mask = x_sb[:, 0:TILES]
        late_mask = x_sb[:, TILES:TILES + GROUPS]

        ps = ctx.enter_context(nc.psum_tensor("ps", [128, 8, BANK], F32))
        def z_ps(par):
            return ps[:, par, 0:GT * D]

        def agg_ps(par):
            return ps[0:D + 1, 2 + par, 0:WIN]
        u_ps = ps[0:D + 1, 7, 0:D]
        wm_ps = ps[0:D + 1, 7, D:2 * D]
        wo_ps = ps[0:D + 1, 7, 2 * D:3 * D]
        in_ps = ps[0:1, 7, 3 * D:3 * D + 1]

        x_in = [sem(f"x_in{k}") for k in range(LCHUNKS)]
        w_in = sem("w_in")
        dst_in = sem("dst_in")
        base_in = sem("base_in")
        iota_ok = sem("iota_ok")
        ident_ok = sem("ident_ok")
        clear_ok = sem("clear_ok")
        acc_clear = sem("acc_clear")
        dve_self = sem("dve_self")
        loop_self = sem("loop_self")
        slow_self = sem("slow_self")
        again_self = sem("again_self")
        xc_ok = sem("xc_ok")
        sq_ok = sem("sq_ok")
        var_ok = sem("var_ok")
        std_ok = sem("std_ok")
        h_ok = sem("h_ok")
        hT_ps_ok = sem("hT_ps_ok")
        hT_ok = sem("hT_ok")
        p_ps_ok = sem("p_ps_ok")
        p_copied = sem("p_copied")
        p_out = [sem(f"p_out{b}") for b in range(2)]
        h_out = sem("h_out")
        wprep_ok = sem("wprep_ok")
        small_ok = sem("small_ok")
        mask_ok = sem("mask_ok")
        flag_ok = sem("flag_ok")
        ea_in = [sem(f"ea_in{b}") for b in range(2)]
        idx_in = [sem(f"idx_in{b}") for b in range(2)]
        raw_in = [sem(f"raw_in{b}") for b in range(RAW)]
        g_in = [sem(f"g_in{s}") for s in range(RING)]
        slot_taken = sem("slot_taken")
        z_ok = sem("z_ok")
        zg_ok = sem("zg_ok")
        er_ok = sem("er_ok")
        s_ok = sem("s_ok")
        hot_ok = sem("hot_ok")
        agg_ok = sem("agg_ok")
        acc_ok = sem("acc_ok")
        slow_step = sem("slow_step")
        slow_tile = sem("slow_tile")
        slow_ea = sem("slow_ea")
        slow_idx = sem("slow_idx")
        slow_g = sem("slow_g")
        slow_z = sem("slow_z")
        slow_zg = sem("slow_zg")
        slow_er = sem("slow_er")
        slow_s = sem("slow_s")
        slow_hot = sem("slow_hot")
        slow_agg = sem("slow_agg")
        slow_acc = sem("slow_acc")

        class NodeSems:
            def __init__(self, pre):
                self.hT_ps = sem(pre + "hT_ps")
                self.hT = sem(pre + "hT")
                self.tot = sem(pre + "tot")
                self.yz = sem(pre + "yz")
                self.y1 = sem(pre + "y1")
                self.er = sem(pre + "er")
                self.v = sem(pre + "v")
                self.vT_ps = sem(pre + "vT_ps")
                self.vT = sem(pre + "vT")
                self.o_ps = sem(pre + "o_ps")
                self.o = sem(pre + "o")

        nd = NodeSems("node_")
        ag = NodeSems("again_")
        node_step = sem("node_step")
        hx_in = [sem(f"hx_in{b}") for b in range(2)]
        o_out = [sem(f"o_out{b}") for b in range(2)]
        again_go = sem("again_go")
        again_hx = sem("again_hx")
        again_out = sem("again_out")

        x_v = x.rearrange("(p t) d -> p (t d)", t=NT)
        P_v = P_dram.rearrange("(p t) d -> p (t d)", t=NT)
        h_v = h_dram.rearrange("(p t) d -> p (t d)", t=NT)
        N_W = 13 * 16
        PARTS = ((0, SPLIT), (SPLIT, NP))

        ln_chunks = [(NP, x_sb[0:NP, k * LT * D:(k + 1) * LT * D].rearrange("p (t d) -> p t d", d=D), LT, False)
                     for k in range(LCHUNKS)]
        ln_chunks += [(128, raw[:, t:min(t + LT, RAW * CHUNK_TILES), :], min(LT, RAW * CHUNK_TILES - t), True)
                      for t in range(0, RAW * CHUNK_TILES, LT)]
        units, first_unit = [], []
        for k, (_, _, n, _) in enumerate(ln_chunks):
            first_unit.append(len(units))
            units += [(k, t, min(QT, n - t)) for t in range(0, n, QT)]
        first_unit.append(len(units))
        TABLE_UNITS = first_unit[LCHUNKS]

        block = ctx.enter_context(nc.Block())

        @block.sync
        def _(sp):
            def load_idx(c, par):
                sp.dma_start(idx[par][:, :], src_t[:, bass.ds(c * CHUNK_TILES, CHUNK_TILES)]).then_inc(idx_in[par], 16)

            def load_edges(c, par):
                sp.dma_start(ea[par][0:D, :], edge_t[bass.ds(c, 1), :, :].rearrange("c d e -> (c d) e")
                             ).then_inc(ea_in[par], 16)

            def load_nodes(m, par, signal):
                for j, t in enumerate((h_dram, x)):
                    sp.dma_start(hx[:, par, j, :], t[bass.ds(m * M, M), :]).then_inc(signal, 16)

            for c in range(RAW):
                load_idx(c, c)
            for k in range(LCHUNKS):
                for a, b in PARTS:
                    sp.dma_start(x_sb[a:b, k * LT * D:(k + 1) * LT * D], x_v[a:b, k * LT * D:(k + 1) * LT * D]
                                 ).then_inc(x_in[k], 16)
            sp.dma_start(base_i[:, :], dst_first.broadcast_to((128, GROUPS))).then_inc(base_in, 16)
            sp.dma_start(dstl[:, :].bitcast(I32), dst_t).then_inc(dst_in, 16)
            load_edges(0, 0)
            load_edges(1, 1)
            for k in range(LCHUNKS):
                cols = slice(k * LT * D, (k + 1) * LT * D)
                sp.wait_ge(h_ok, k + 1)
                for a, b in PARTS:
                    sp.dma_start(h_v[a:b, cols], x_sb[a:b, cols]).then_inc(h_out, 16)
                sp.wait_ge(p_copied, first_unit[k + 1])
                for a, b in PARTS:
                    sp.dma_start(P_v[a:b, cols], P_st[a:b, k % 2, :, :].rearrange("p t d -> p (t d)")
                                 ).then_inc(p_out[k % 2], 16)

            def step(c, par, n, waits=True, next_idx=True):
                if next_idx:
                    if waits:
                        sp.wait_ge(g_in[(1 - par) * CG + CG - 1], n * (16 * GT))
                    load_idx(c + 1, 1 - par)
                sp.wait_ge(z_ok, (c - 1) * CG)
                load_edges(c, par)
                if waits:
                    sp.wait_ge(nd.o, c - 3)
                load_nodes(c - 2, par, hx_in[par])

            sp.wait_ge(raw_in[0], 16 * CHUNK_TILES)
            load_idx(2, 0)
            sp.wait_ge(raw_in[1], 16 * CHUNK_TILES)
            load_idx(3, 1)
            sp.wait_ge(h_out, LCHUNKS * 32)
            step(2, 0, 0, waits=False, next_idx=False)
            sp.wait_ge(g_in[CG - 1], 16 * GT)
            load_idx(4, 0)
            step(3, 1, 0, waits=False, next_idx=False)
            with sp.Fori(0, (CHUNKS - 5) // 2) as i:
                step(i * 2 + 4, 0, i + 1)
                step(i * 2 + 5, 1, i + 2)
            step(CHUNKS - 1, 0, 0, next_idx=False)
            for m in (CHUNKS - 2, CHUNKS - 1):
                sp.wait_ge(nd.o, m - 1)
                load_nodes(m, m % 2, hx_in[m % 2])

            sp.wait_ge(flag_ok, 1)
            with sp.If(sp.value_load(flag[0:1, 0:1], min_val=0, max_val=2 * EDGES) != 0):
                with sp.Fori(0, CHUNKS) as c:
                    with sp.Fori(0, CHUNK_TILES) as k:
                        t = c * CHUNK_TILES + k
                        sp.wait_ge(slow_tile, t + 1)
                        sp.sem_inc(slow_step, 1)
                        sp.dma_start(idx[0][:, 0:1], src_t[:, bass.ds(t, 1)], allow_slow_non_contiguous=True
                                     ).then_inc(slow_idx, 16)
                        sp.dma_start(ea[0][0:D, 0:TILE],
                                     edge_t[bass.ds(c, 1), :, bass.ds(k * TILE, TILE)].rearrange("c d e -> (c d) e")
                                     ).then_inc(slow_ea, 16)
            with sp.If(sp.value_load(flag[0:1, 1:2], min_val=0, max_val=2 * EDGES) != 0):
                with sp.Fori(0, CHUNKS) as m:
                    sp.wait_ge(again_go, m + 1)
                    load_nodes(m, 0, again_hx)

        @block.gpsimd
        def _(pool):
            def gather(dst_rows, table, par, tile, signal):
                pool.indirect_dma_start(dst_rows, None, table,
                                        bass.IndirectOffsetOnAxis(idx[par][:, tile:tile + 1], 0)).then_inc(signal, 16)

            nc.gpsimd.memset(ident[:, :], 0.0).then_inc(ident_ok, 1)
            pool.wait_ge(ident_ok, 1)
            nc.gpsimd.affine_select(out=ident[:, :], in_=ident[:, :], compare_op=ALU.not_equal, fill=1.0, base=0,
                                    pattern=[[-1, 128]], channel_multiplier=1).then_inc(ident_ok, 1)
            for c in range(RAW):
                pool.wait_ge(idx_in[c], 16)
                for t in range(CHUNK_TILES):
                    gather(raw[:, c * CHUNK_TILES + t, :], x, c, t, raw_in[c])
            nc.gpsimd.iota(iota_i[:, :], [[1, WIDE]], base=0, channel_multiplier=0).then_inc(iota_ok, 1)
            nc.gpsimd.iota(due_i[:, :], [[M, CHUNKS], [0, CG]], base=-M, channel_multiplier=0).then_inc(iota_ok, 1)
            pool.wait_ge(p_out[0], 32 * ((LCHUNKS + 1) // 2))
            pool.wait_ge(p_out[1], 32 * (LCHUNKS // 2))

            def gather_chunk(c, par, loads, first=False):
                pool.wait_ge(idx_in[par], loads * 16)
                pool.sem_inc(slot_taken, 1)
                for q in range(CG):
                    if not first:
                        pool.wait_ge(zg_ok, c * CG + (q + 1 - RING))
                        pool.sem_inc(slot_taken, 1)
                    s = par * CG + q
                    for t in range(GT):
                        gather(G[:, s, t * D:(t + 1) * D], P_dram, par, q * GT + t, g_in[s])

            gather_chunk(2, 0, 2, first=True)
            gather_chunk(3, 1, 2, first=True)
            with pool.Fori(0, (CHUNKS - 5) // 2) as i:
                gather_chunk(i * 2 + 4, 0, i + 3)
                gather_chunk(i * 2 + 5, 1, i + 3)
            gather_chunk(CHUNKS - 1, 0, (CHUNKS + 1) // 2)

            pool.wait_ge(flag_ok, 1)
            with pool.If(pool.value_load(flag[0:1, 0:1], min_val=0, max_val=2 * EDGES) != 0):
                with pool.Fori(0, TILES) as t:
                    pool.wait_ge(slow_tile, t + 1)
                    pool.wait_ge(slow_idx, (t + 1) * 16)
                    pool.sem_inc(slow_step, 1)
                    gather(G[:, 0, 0:D], P_dram, 0, 0, slow_g)

        @block.scalar
        def _(act):
            act.sem_inc(o_out[0], 16)
            act.sem_inc(o_out[1], 16)
            act.sem_inc(again_out, 16)
            act.wait_ge(clear_ok, 1)
            for dst_ap, src_ap in (
                (W_pair[0:D, 0:D], W1a[0:D, :]), (W_pair[D:2 * D, D:2 * D], W1a[0:D, :]),
                (b1a_rows[:, :], b1a.broadcast_to((128, D))), (W_h[0:D, :], W2a[0:D, :]), (W_h[D:D + 1, :], b2a),
                (L_u0[:, D:D + 1], u0), (W2g[:, :], W2a[2 * D:3 * D, :]), (W_edge[:, :], W1a[D:2 * D, :]),
                (W2m[:, :], W2a[D:2 * D, :]), (W1bT_s[:, :], W1bT), (b1b_s[:, :], b1b), (W2b_s[:, :], W2b),
                (W_out[D:D + 1, :], b2b),
            ):
                act.dma_start(dst_ap, src_ap).then_inc(w_in, 16)

            def square(k):
                rows, tiles, n, _ = ln_chunks[k]
                act.wait_ge(xc_ok, k + 1)
                if k >= 2:
                    act.wait_ge(var_ok, k - 1)
                nc.scalar.activation(sq[0:rows, k % 2, 0:n, :], tiles, ACT.Square).then_inc(sq_ok, 1)
                act.wait_ge(var_ok, k + 1)
                nc.scalar.activation(stat[0:rows, 2, 0:n], stat[0:rows, 1, 0:n], ACT.Sqrt, bias=eps[0:rows, :],
                                     scale=1.0 / D).then_inc(std_ok, 1)

            square(0)
            part = ACC_COLS // LCHUNKS
            for k in range(len(ln_chunks)):
                if k + 1 < len(ln_chunks):
                    square(k + 1)
                if k < LCHUNKS:
                    nc.scalar.copy(acc[:, k * part:(k + 1) * part], zero[:, :].broadcast_to((128, part))
                                   ).then_inc(acc_clear, 1)
                for n in range(first_unit[k], first_unit[k + 1]):
                    act.wait_ge(hT_ps_ok, n + 1)
                    if n >= 2:
                        act.wait_ge(p_ps_ok, n - 1)
                    used = units[n][2] // 2 * ln_chunks[k][0]
                    nc.scalar.copy(hT[:, n % 2, 0:used], ps[:, n % 2, 0:used]).then_inc(hT_ok, 1)

            def exp_relu(c, par, q, first=False):
                slot = (par + q) % 2
                act.wait_ge(zg_ok, c * CG + (q + 1))
                if not (first and q < 2):
                    act.wait_ge(s_ok, c * CG + (q - 1))
                nc.scalar.activation(E[:, slot, :], Z[:, slot, :], ACT.Exp, bias=ln_alpha[:, :])
                nc.scalar.activation(Z[:, slot, :], Z[:, slot, :], ACT.Relu).then_inc(er_ok, 1)

            def node_hT(m, w):
                act.wait_ge(w.hT_ps, m + 1)
                nc.scalar.copy(nhT[0:D, :], ps[0:D, 4, 0:M]).then_inc(w.hT, 1)

            def node_exp(m, w):
                act.wait_ge(w.y1, m + 1)
                nc.scalar.activation(y_exp[:, :], y[:, :], ACT.Exp, bias=ln_alpha[0:M, :])
                nc.scalar.activation(y[:, :], y[:, :], ACT.Relu).then_inc(w.er, 1)

            def node_vT(m, w):
                act.wait_ge(w.vT_ps, m + 1)
                nc.scalar.copy(nvT[0:D, :], ps[0:D, 6, 0:M]).then_inc(w.vT, 1)

            def node_store(m, par, w, signal):
                act.wait_ge(w.o, m + 1)
                act.dma_start(out[bass.ds(m * M, M), :], o_st[:, par, :]).then_inc(signal, 16)

            def chunk(c, par):
                m = c - 2
                exp_relu(c, par, 0)
                node_hT(m, nd)
                exp_relu(c, par, 1)
                exp_relu(c, par, 2)
                node_exp(m, nd)
                exp_relu(c, par, 3)
                node_vT(m, nd)
                exp_relu(c, par, 4)
                node_store(m, par, nd, o_out[par])

            for c in range(RAW):
                for q in range(CG):
                    exp_relu(c, c, q, first=c == 0)
            with act.Fori(0, (CHUNKS - 3) // 2) as i:
                chunk(i * 2 + 2, 0)
                chunk(i * 2 + 3, 1)
            chunk(CHUNKS - 1, 0)

            act.wait_ge(flag_ok, 1)
            with act.If(act.value_load(flag[0:1, 0:1], min_val=0, max_val=2 * EDGES) != 0):
                with act.Fori(0, TILES) as t:
                    act.wait_ge(slow_zg, t + 1)
                    nc.scalar.activation(E[:, 0, 0:D], Z[:, 0, 0:D], ACT.Exp, bias=ln_alpha[:, :])
                    nc.scalar.activation(Z[:, 0, 0:D], Z[:, 0, 0:D], ACT.Relu).then_inc(slow_er, 1)

            def node_tile(m, par, w, signal):
                node_hT(m, w)
                node_exp(m, w)
                node_vT(m, w)
                node_store(m, par, w, signal)

            for m in (CHUNKS - 2, CHUNKS - 1):
                node_tile(m, m % 2, nd, o_out[m % 2])
            for b in range(2):
                act.wait_ge(o_out[b], 16 + 16 * ((CHUNKS + 1 - b) // 2))
            with act.If(act.value_load(flag[0:1, 1:2], min_val=0, max_val=2 * EDGES) != 0):
                with act.Fori(0, CHUNKS) as m:
                    node_tile(m, 0, ag, again_out)
                act.wait_ge(again_out, 16 + 16 * CHUNKS)

        @block.vector
        def _(dve):
            steps = {dve_self: 0, slow_self: 0}

            def link(ins, s=dve_self):
                steps[s] += 1
                ins.then_inc(s, 1)
                dve.wait_ge(s, steps[s])

            def over_tiles(col, rows, n):
                return col.rearrange("p (t o) -> p t o", o=1).broadcast_to((rows, n, D))

            nc.vector.memset(W_pair[:, :], 0.0)
            nc.vector.memset(L_u0[:, :], 0.0)
            nc.vector.memset(L_one[:, :], 0.0)
            nc.vector.memset(W_mean[:, :], 0.0)
            nc.vector.memset(ln_alpha[:, :], float(np.log(ALPHA)))
            nc.vector.memset(eps[:, :], EPS)
            nc.vector.memset(zero[:, :], 0.0)
            nc.vector.memset(one[:, :], 1.0)
            nc.vector.memset(nhT[D:D + 1, :], 1.0)
            nc.vector.memset(nvT[D:D + 1, :], 1.0)
            link(nc.vector.memset(S[:, :, :, D:D + 1], 1.0))
            nc.vector.memset(L_one[:, D:D + 1], 1.0)
            nc.vector.memset(W_mean[D:D + 1, D:D + 1], 1.0).then_inc(clear_ok, 1)

            def normalise(k):
                rows, h, n, gathered = ln_chunks[k]
                if gathered:
                    for c in range(RAW):
                        dve.wait_ge(raw_in[c], 16 * CHUNK_TILES)
                else:
                    dve.wait_ge(x_in[k], 32)
                st = stat[0:rows, :, 0:n]
                link(nc.vector.tensor_reduce(out=st[:, 0, :], in_=h, op=ALU.add, axis=AX.X))
                link(nc.vector.tensor_scalar(st[:, 3, :], st[:, 0, :], -1.0 / D, None, ALU.mult))
                nc.vector.tensor_tensor(h, h, over_tiles(st[:, 3, :], rows, n), ALU.add).then_inc(xc_ok, 1)
                dve.wait_ge(sq_ok, k + 1)
                nc.vector.tensor_reduce(out=st[:, 1, :], in_=sq[0:rows, k % 2, 0:n, :], op=ALU.add, axis=AX.X
                                        ).then_inc(var_ok, 1)
                dve.wait_ge(std_ok, k + 1)
                link(nc.vector.reciprocal(st[:, 3, :], st[:, 2, :]))
                nc.vector.scalar_tensor_tensor(out=h, in0=h, scalar=0.0, in1=over_tiles(st[:, 3, :], rows, n),
                                               op0=ALU.max, op1=ALU.mult).then_inc(h_ok, 1)

            def copy_p(n):
                k, t0, nt = units[n]
                rows, tiles, _, gathered = ln_chunks[k]
                to = tiles if gathered else P_st[:, k % 2, :, :]
                if not gathered and k >= 2 and t0 == 0:
                    dve.wait_ge(p_out[k % 2], 32 * (k // 2))
                dve.wait_ge(p_ps_ok, n + 1)
                nc.vector.tensor_tensor(
                    to[:, t0:t0 + nt, :], ps[0:rows, 2 + n % 2, 0:nt * D].rearrange("p (t d) -> p t d", d=D),
                    b1a_rows[0:rows, :].rearrange("p (o d) -> p o d", o=1).broadcast_to((rows, nt, D)), ALU.add
                ).then_inc(p_copied, 1)

            def prepare_weights():
                link(nc.vector.tensor_reduce(out=rs[:, 0:1], in_=W1bT_s[:, :], op=ALU.add, axis=AX.X))
                nc.vector.scalar_tensor_tensor(out=L_mean[:, D:D + 1], in0=rs[:, 0:1], scalar=-ALPHA * LAM,
                                               in1=b1b_s[:, :], op0=ALU.mult, op1=ALU.add)
                nc.vector.tensor_scalar(L_mean[:, 0:D], W1bT_s[:, :], LAM, None, ALU.mult)
                nc.vector.tensor_scalar(W_out[0:D, :], W2b_s[:, :], LAM, None, ALU.mult).then_inc(wprep_ok, 1)
                dve.wait_ge(small_ok, 3)
                nc.vector.tensor_copy(W_mean[:, 0:D], wm_ps)
                nc.vector.scalar_tensor_tensor(out=W_out[D:D + 1, :], in0=wo_ps[D:D + 1, :], scalar=-ALPHA * LAM,
                                               in1=W_out[D:D + 1, :], op0=ALU.mult, op1=ALU.add)
                nc.vector.tensor_tensor(W_h[D:D + 1, :], W_h[D:D + 1, :], u_ps[D:D + 1, :], ALU.add).then_inc(wprep_ok, 1)

            normalise(0)
            for k in range(len(ln_chunks)):
                if k + 1 < len(ln_chunks):
                    normalise(k + 1)
                if k == 0:
                    dve.wait_ge(w_in, N_W)
                for n in range(first_unit[k], first_unit[k + 1]):
                    copy_p(n)
                if k == LCHUNKS - 1:
                    prepare_weights()
                    dve.wait_ge(base_in, 16)
                    dve.wait_ge(dst_in, 16)
                    nc.vector.tensor_tensor(
                        dstl[:, :].rearrange("p (g t) -> p g t", t=GT),
                        dstl[:, :].bitcast(I32).rearrange("p (g t) -> p g t", t=GT),
                        base_i[:, :].rearrange("p (g o) -> p g o", o=1).broadcast_to((128, GROUPS, GT)), ALU.subtract)
                    dve.wait_ge(iota_ok, 2)
                    link(nc.vector.tensor_copy(iota[:, :], iota_i[:, :]))
            dve.wait_ge(acc_clear, LCHUNKS)

            def add_window(g, par):
                base = dve.value_load(base_i[0:1, bass.ds(g, 1)], min_val=0, max_val=NODES - 1)
                dve.wait_ge(agg_ok, g + 1)
                window = acc[0:D + 1, bass.ds(base, WIN)]
                nc.vector.tensor_tensor(window, window, agg_ps(par), ALU.add).then_inc(acc_ok, 1)

            def combine(c, par, q, first=False):
                rows = raw[:, c * CHUNK_TILES + q * GT:c * CHUNK_TILES + (q + 1) * GT, :].rearrange("p t d -> p (t d)") \
                    if isinstance(c, int) and c < RAW else G[:, par * CG + q, :]
                slot = (par + q) % 2
                if not first:
                    dve.wait_ge(agg_ok, c * CG + (q + 1 - CG))
                nc.vector.tensor_tensor(
                    hot[:, q, :, :], iota[:, 0:WIN].rearrange("p (o w) -> p o w", o=1).broadcast_to((128, GT, WIN)),
                    dstl[:, bass.ds(c * CHUNK_TILES + q * GT, GT)].rearrange("p (t o) -> p t o", o=1).broadcast_to(
                        (128, GT, WIN)), ALU.is_equal).then_inc(hot_ok, 1)
                if not (isinstance(c, int) and c < RAW):
                    dve.wait_ge(g_in[par * CG + q], gathers(c, par) * (16 * GT))
                dve.wait_ge(z_ok, c * CG + (q + 1))
                nc.vector.tensor_tensor(Z[:, slot, :], rows, z_ps(slot), ALU.add).then_inc(zg_ok, 1)
                dve.wait_ge(er_ok, c * CG + (q + 1))
                nc.vector.scalar_tensor_tensor(
                    out=S[:, q, :, 0:D], in0=E[:, slot, :].rearrange("p (t d) -> p t d", d=D), scalar=ALPHA,
                    in1=Z[:, slot, :].rearrange("p (t d) -> p t d", d=D), op0=ALU.min, op1=ALU.add).then_inc(s_ok, 1)
                if not (first and q == 0):
                    if not (first and q == 1):
                        dve.wait_ge(acc_ok, c * CG + (q - 1))
                    add_window(c * CG + (q - 1), (par + q + 1) % 2)

            turn = [None]

            def gathers(c, par):
                return (CHUNKS - 1) // 2 if isinstance(c, int) else turn[0] + 1

            def node_totals(m, w):
                nc.vector.tensor_copy(tot[:, :], acc[0:D + 1, bass.ds(m * M, M)]).then_inc(w.tot, 1)

            def node_first(m, w, own):
                dve.wait_ge(w.yz, m + 1)
                nc.vector.tensor_scalar(rc[:, 0:1], ps[0:M, 5, 2 * D:2 * D + 1], 1.0, None, ALU.max).then_inc(own, 1)
                dve.wait_ge(own, m * 3 + 1)
                nc.vector.reciprocal(rc[:, 1:2], rc[:, 0:1]).then_inc(own, 1)
                dve.wait_ge(own, m * 3 + 2)
                nc.vector.tensor_scalar(y[:, :], ps[0:M, 5, D:2 * D], rc[:, 1:2], None, ALU.mult).then_inc(own, 1)
                dve.wait_ge(own, m * 3 + 3)
                nc.vector.tensor_tensor(y[:, :], y[:, :], ps[0:M, 5, 0:D], ALU.add).then_inc(w.y1, 1)

            def node_s(m, w):
                dve.wait_ge(w.er, m + 1)
                nc.vector.scalar_tensor_tensor(out=y[:, :], in0=y_exp[:, :], scalar=ALPHA, in1=y[:, :],
                                               op0=ALU.min, op1=ALU.add).then_inc(w.v, 1)

            def node_out(m, par, w, out_sem, stores):
                dve.wait_ge(out_sem, (stores + 1) * 16)
                dve.wait_ge(w.o_ps, m + 1)
                nc.vector.tensor_tensor(o_st[:, par, :], ps[0:M, 7, 0:D], hx[:, par, 1, :], ALU.add).then_inc(w.o, 1)

            def chunk(c, par, stores):
                m = c - 2
                combine(c, par, 0)
                dve.wait_ge(acc_ok, c * CG)
                node_totals(m, nd)
                combine(c, par, 1)
                node_first(m, nd, loop_self)
                combine(c, par, 2)
                node_s(m, nd)
                combine(c, par, 3)
                combine(c, par, 4)
                dve.wait_ge(hx_in[par], (stores + 1) * 32)
                node_out(m, par, nd, o_out[par], stores)

            for c in range(RAW):
                for q in range(CG):
                    combine(c, c, q, first=c == 0)

            nc.vector.tensor_tensor(late_mask, base_i[:, :], due_i[:, :], ALU.is_lt)
            link(nc.vector.tensor_scalar(in_mask, dstl[:, :], 0.0, None, ALU.is_ge))
            nc.vector.tensor_reduce(out=late[:, :], in_=late_mask, op=ALU.add, axis=AX.X)
            link(nc.vector.scalar_tensor_tensor(out=in_mask, in0=dstl[:, :], scalar=float(WIN), in1=in_mask,
                                                op0=ALU.is_lt, op1=ALU.mult))
            nc.vector.tensor_reduce(out=inside[:, :], in_=in_mask, op=ALU.add, axis=AX.X).then_inc(mask_ok, 1)
            dve.wait_ge(small_ok, 4)
            link(nc.vector.tensor_scalar(flag_f[:, :], in_ps, -1.0, float(EDGES), ALU.mult, ALU.add))
            nc.vector.tensor_copy(flag[:, 0:1], flag_f[:, :])
            nc.vector.tensor_tensor(flag[:, 1:2], flag_f[:, :], late[0:1, :], ALU.add).then_inc(flag_ok, 1)

            with dve.Fori(0, (CHUNKS - 3) // 2) as i:
                turn[0] = i
                chunk(i * 2 + 2, 0, i)
                chunk(i * 2 + 3, 1, i)
            chunk(CHUNKS - 1, 0, (CHUNKS - 3) // 2)
            dve.wait_ge(acc_ok, GROUPS - 1)
            add_window(GROUPS - 1, (GROUPS - 1) % 2)
            dve.wait_ge(acc_ok, GROUPS)

            with dve.If(dve.value_load(flag[0:1, 0:1], min_val=0, max_val=2 * EDGES) != 0):
                base_b = base_i[:, :].rearrange("p (g o) -> p g o", o=1).broadcast_to((128, GROUPS, GT))
                as_groups = lambda a: a.rearrange("p (g t) -> p g t", t=GT)
                link(nc.vector.tensor_tensor(as_groups(dstl[:, :]), as_groups(dstl[:, :]), base_b, ALU.add), slow_self)
                nc.vector.scalar_tensor_tensor(out=dstl[:, :], in0=in_mask, scalar=-2.0 * ACC_COLS, in1=dstl[:, :],
                                               op0=ALU.mult, op1=ALU.add).then_inc(slow_tile, 1)
                dve.wait_ge(slow_tile, 1)
                nc.vector.tensor_copy(kv[:, :], dstl[:, 0:1]).then_inc(slow_acc, 1)
                with dve.Fori(0, TILES) as t:
                    dve.wait_ge(slow_g, (t + 1) * 16)
                    dve.wait_ge(slow_z, t + 1)
                    nc.vector.tensor_tensor(Z[:, 0, 0:D], G[:, 0, 0:D], ps[:, 0, 0:D], ALU.add).then_inc(slow_zg, 1)
                    dve.wait_ge(slow_er, t + 1)
                    nc.vector.scalar_tensor_tensor(out=S[:, 0, 0, 0:D], in0=E[:, 0, 0:D], scalar=ALPHA, in1=Z[:, 0, 0:D],
                                                   op0=ALU.min, op1=ALU.add).then_inc(slow_s, 1)
                    dve.wait_ge(slow_acc, t * WIDES + 1)
                    nc.vector.tensor_copy(kv[:, :], dstl[:, bass.ds(t, 1)]).then_inc(slow_s, 1)
                    dve.wait_ge(slow_s, (t + 1) * 2)
                    dve.sem_inc(slow_step, 1)
                    with dve.Fori(0, WIDES) as v:
                        n = t * WIDES + v
                        dve.wait_ge(slow_acc, n + 1)
                        nc.vector.tensor_scalar(hot_wide, iota[:, :], kv[:, 0:1], None, ALU.is_equal).then_inc(slow_hot, 1)
                        dve.wait_ge(slow_agg, n + 1)
                        nc.vector.tensor_scalar(kv[:, :], kv[:, :], -float(WIDE), None, ALU.add)
                        wide = acc[0:D + 1, bass.ds(v * WIDE, WIDE)]
                        nc.vector.tensor_tensor(wide, wide, ps[0:D + 1, 2, :], ALU.add).then_inc(slow_acc, 1)
                    dve.wait_ge(slow_acc, t * WIDES + (WIDES + 1))
                    dve.sem_inc(slow_tile, 1)

            for m in (CHUNKS - 2, CHUNKS - 1):
                node_totals(m, nd)
                node_first(m, nd, loop_self)
                node_s(m, nd)
                dve.wait_ge(hx_in[m % 2], (m // 2 + 1) * 32)
                node_out(m, m % 2, nd, o_out[m % 2], m // 2)

            with dve.If(dve.value_load(flag[0:1, 1:2], min_val=0, max_val=2 * EDGES) != 0):
                for b in range(2):
                    dve.wait_ge(o_out[b], 16 + 16 * ((CHUNKS + 1 - b) // 2))
                dve.sem_inc(again_go, 1)
                with dve.Fori(0, CHUNKS) as m:
                    node_totals(m, ag)
                    node_first(m, ag, again_self)
                    node_s(m, ag)
                    dve.wait_ge(again_hx, (m + 1) * 32)
                    node_out(m, 0, ag, again_out, m)
                    dve.wait_ge(ag.o, m + 1)
                    dve.sem_inc(again_go, 1)

        @block.tensor
        def _(pe):
            mm = nc.tensor.matmul
            pe.wait_ge(ident_ok, 2)
            pe.wait_ge(w_in, N_W)

            def products(n):
                k, _, nt = units[n]
                rows = ln_chunks[k][0]
                pe.wait_ge(hT_ok, n + 1)
                if n >= 2:
                    pe.wait_ge(p_copied, n - 1)
                for p in range(nt // 2):
                    last = mm(ps[0:rows, 2 + n % 2, p * 2 * D:(p + 1) * 2 * D], hT[:, n % 2, p * rows:(p + 1) * rows],
                              W_pair[:, :], start=True, stop=True)
                last.then_inc(p_ps_ok, 1)

            for n, (k, t0, nt) in enumerate(units):
                rows, tiles, _, _ = ln_chunks[k]
                pe.wait_ge(h_ok, k + 1)
                if n >= 2:
                    pe.wait_ge(hT_ok, n - 1)
                for p in range(nt // 2):
                    pair = tiles[:, t0 + 2 * p:t0 + 2 * p + 2, :].rearrange("p t d -> p (t d)")
                    last = nc.tensor.transpose(ps[:, n % 2, p * rows:(p + 1) * rows], pair, ident[0:rows, 0:rows])
                last.then_inc(hT_ps_ok, 1)
                if n >= 1:
                    products(n - 1)
                if n == TABLE_UNITS:
                    pe.wait_ge(wprep_ok, 1)
                    mm(u_ps, L_u0[:, :], W2g[:, :], start=True, stop=True).then_inc(small_ok, 1)
                    mm(wm_ps, L_mean[:, :], W2m[:, :], start=True, stop=True).then_inc(small_ok, 1)
                    mm(wo_ps, L_one[:, :], W2b_s[:, :], start=True, stop=True).then_inc(small_ok, 1)
            products(len(units) - 1)
            pe.wait_ge(wprep_ok, 2)
            pe.wait_ge(p_copied, len(units))

            def sum_group(c, par, q, first=False):
                pq = (q - 1) % CG
                pe.wait_ge(s_ok, c * CG + q)
                pe.wait_ge(hot_ok, c * CG + q)
                if not (first and q < 3):
                    pe.wait_ge(acc_ok, c * CG + (q - 2))
                for t in range(GT):
                    last = mm(agg_ps((par + q + 1) % 2), S[:, pq, t, :], hot[:, pq, t, :], start=(t == 0), stop=(t == GT - 1))
                last.then_inc(agg_ok, 1)

            def edge_group(c, par, loads, q, first=False):
                slot = (par + q) % 2
                if q == 0:
                    pe.wait_ge(ea_in[par], loads * 16)
                if not (first and q < 2):
                    pe.wait_ge(zg_ok, c * CG + (q - 1))
                for t in range(GT):
                    e0 = (q * GT + t) * TILE
                    last = mm(z_ps(slot)[:, t * D:(t + 1) * D], ea[par][0:D, e0:e0 + TILE], W_edge[:, :],
                              start=True, stop=True)
                last.then_inc(z_ok, 1)
                if not (first and q == 0):
                    sum_group(c, par, q, first)

            def node_hT(m, par, w, hx_sem, loads):
                pe.wait_ge(hx_sem, loads * 32)
                pe.sem_inc(node_step, 1)
                nc.tensor.transpose(ps[0:D, 4, 0:M], hx[:, par, 0, :], ident[0:M, 0:M]).then_inc(w.hT_ps, 1)

            def node_first(m, w):
                pe.wait_ge(w.hT, m + 1)
                pe.wait_ge(w.tot, m + 1)
                mm(ps[0:M, 5, 0:D], nhT[:, :], W_h[:, :], start=True, stop=True)
                mm(ps[0:M, 5, D:2 * D + 1], tot[:, :], W_mean[:, :], start=True, stop=True).then_inc(w.yz, 1)

            def node_vT(m, w):
                pe.wait_ge(w.v, m + 1)
                pe.sem_inc(node_step, 1)
                nc.tensor.transpose(ps[0:D, 6, 0:M], y[:, :], ident[0:M, 0:M]).then_inc(w.vT_ps, 1)

            def node_out(m, w):
                pe.wait_ge(w.vT, m + 1)
                mm(ps[0:M, 7, 0:D], nvT[:, :], W_out[:, :], start=True, stop=True).then_inc(w.o_ps, 1)

            def chunk(c, par, loads):
                m = c - 2
                edge_group(c, par, loads, 0)
                node_hT(m, par, nd, hx_in[par], loads - 1)
                edge_group(c, par, loads, 1)
                node_first(m, nd)
                edge_group(c, par, loads, 2)
                edge_group(c, par, loads, 3)
                node_vT(m, nd)
                edge_group(c, par, loads, 4)
                node_out(m, nd)

            for c in range(RAW):
                for q in range(CG):
                    edge_group(c, c, 1, q, first=c == 0)
            pe.wait_ge(mask_ok, 1)
            mm(in_ps, inside[:, :], one[:, :], start=True, stop=True).then_inc(small_ok, 1)
            with pe.Fori(0, (CHUNKS - 3) // 2) as i:
                chunk(i * 2 + 2, 0, i + 2)
                chunk(i * 2 + 3, 1, i + 2)
            chunk(CHUNKS - 1, 0, (CHUNKS + 1) // 2)
            sum_group(CHUNKS, CHUNKS % 2, 0)

            pe.wait_ge(flag_ok, 1)
            with pe.If(pe.value_load(flag[0:1, 0:1], min_val=0, max_val=2 * EDGES) != 0):
                with pe.Fori(0, TILES) as t:
                    pe.wait_ge(slow_ea, (t + 1) * 16)
                    mm(ps[:, 0, 0:D], ea[0][0:D, 0:TILE], W_edge[:, :], start=True, stop=True).then_inc(slow_z, 1)
                    pe.wait_ge(slow_s, (t + 1) * 2)
                    pe.sem_inc(slow_step, 1)
                    with pe.Fori(0, WIDES) as v:
                        pe.wait_ge(slow_hot, t * WIDES + v + 1)
                        mm(ps[0:D + 1, 2, :], S[:, 0, 0, :], hot_wide, start=True, stop=True).then_inc(slow_agg, 1)

            def node_tile(m, par, w, hx_sem, loads):
                node_hT(m, par, w, hx_sem, loads)
                node_first(m, w)
                node_vT(m, w)
                node_out(m, w)

            for m in (CHUNKS - 2, CHUNKS - 1):
                node_tile(m, m % 2, nd, hx_in[m % 2], m // 2 + 1)
            with pe.If(pe.value_load(flag[0:1, 1:2], min_val=0, max_val=2 * EDGES) != 0):
                with pe.Fori(0, CHUNKS) as m:
                    node_tile(m, 0, ag, again_hx, m + 1)


def kernel(x, src, dst, edge_attr_64, L0_gnn_u, L0_gnn_W1a, L0_gnn_b1a, L0_gnn_W1b, L0_gnn_b1b, L0_gnn_W2a, L0_gnn_b2a,
           L0_gnn_W2b, L0_gnn_b2b):
    import concourse.bacc as bacc
    from concourse.bass_utils import run_bass_kernel_spmd

    a = np.asarray
    arrays = {
        "x": a(x),
        "src_t": np.ascontiguousarray(a(src).reshape(TILES, TILE).T),
        "dst_t": np.ascontiguousarray(a(dst).reshape(TILES, TILE).T),
        "dst_first": np.ascontiguousarray(a(dst).reshape(GROUPS, GT * TILE)[:, 0].reshape(1, GROUPS)),
        "edge_t": np.ascontiguousarray(a(edge_attr_64).reshape(CHUNKS, CE, D).transpose(0, 2, 1)),
        "u0": np.ascontiguousarray(a(L0_gnn_u)[0].reshape(D, 1)),
        "W1a": a(L0_gnn_W1a),
        "b1a": a(L0_gnn_b1a).reshape(1, D),
        "W1bT": np.ascontiguousarray(a(L0_gnn_W1b).T),
        "b1b": a(L0_gnn_b1b).reshape(D, 1),
        "W2a": a(L0_gnn_W2a),
        "b2a": a(L0_gnn_b2a).reshape(1, D),
        "W2b": a(L0_gnn_W2b),
        "b2b": a(L0_gnn_b2b).reshape(1, D),
    }
    nc = bacc.Bacc("TRN2", target_bir_lowering=False, num_devices=1)
    args = [nc.dram_tensor(name, v.shape, mybir.dt.from_np(v.dtype), kind="ExternalInput").ap() for name, v in arrays.items()]
    out = nc.dram_tensor("out", (NODES, D), F32, kind="ExternalOutput").ap()
    build(nc, *args, out)
    r = run_bass_kernel_spmd(nc, [arrays], core_ids=[0])
    return r.results[0]["out"]
```

```python
from contextlib import ExitStack

import numpy as np
import concourse.bass as bass
from concourse import mybir
from concourse.alu_op_type import AluOpType as ALU

F32 = mybir.dt.float32
I32 = mybir.dt.int32
ACT = mybir.ActivationFunctionType
AX = mybir.AxisListType

ALPHA = 1.6732632423543772
LAM = 1.0507009873554805
EPS = 1e-5

D = 64
NODES = 12500
NP, NT = 125, 100
SPLIT = 112
EDGES = 400000
TILE = 128
TILES = EDGES // TILE
GT = 5
CG = 5
CHUNK_TILES = GT * CG
CHUNKS = TILES // CHUNK_TILES
GROUPS = TILES // GT
CE = CHUNK_TILES * TILE
RAW = 2
RING = 2 * CG
WIN = 32
WIDE = 512
WIDES = -(-NODES // WIDE)
ACC_COLS = WIDES * WIDE
BANK = 512
LN_TILES = (12, 20, 24, 24, 20)
assert sum(LN_TILES) == NT
RAW_TILES = (24, 16, 10)
assert sum(RAW_TILES) == RAW * CHUNK_TILES
LT = max(LN_TILES + RAW_TILES)
LCHUNKS = len(LN_TILES)
QT = 4
M = NODES // CHUNKS
assert M * CHUNKS == NODES and M <= 128


def build(nc, x, src_t, dst_t, dst_first, edge_t, u0, W1a, b1a, W1bT, b1b, W2a, b2a, W2b, b2b, out):
    P_dram = nc.dram_tensor("message_table", (NODES, D), F32, kind="Internal").ap()
    h_dram = nc.dram_tensor("normed", (NODES, D), F32, kind="Internal").ap()

    with ExitStack() as ctx:
        def sb(name, shape, dt=F32):
            return ctx.enter_context(nc.sbuf_tensor(name, shape, dt))

        def sem(name):
            return ctx.enter_context(nc.semaphore(name))

        x_sb = sb("x_sb", [128, NT * D])
        raw = sb("raw", [128, RAW * CHUNK_TILES, D])
        sq = sb("sq", [128, 2, LT, D])
        P_st = sb("P_st", [NP, 2, LT, D])
        hT = sb("hT", [128, 2, QT // 2 * 128])
        stat = sb("stat", [128, 2, 4, LT])
        acc = sb("acc", [128, ACC_COLS])
        dstl = sb("dstl", [128, TILES])
        base_i = sb("base_i", [128, GROUPS], I32)
        due_i = sb("due_i", [128, GROUPS], I32)
        ea = [sb(f"ea{b}", [128, CE]) for b in range(2)]
        idx = [sb(f"idx{b}", [128, CHUNK_TILES], I32) for b in range(2)]
        G = sb("G", [128, RING, GT * D])
        Z = sb("Z", [128, 2, GT * D])
        E = sb("E", [128, 2, GT * D])
        S = sb("S", [128, CG, GT, D + 1])
        hot = sb("hot", [128, CG, GT, WIN])
        iota_i = sb("iota_i", [128, WIDE], I32)
        iota = sb("iota", [128, WIDE])
        ident = sb("ident", [128, 128])
        ln_alpha = sb("ln_alpha", [128, 1])
        eps = sb("eps", [128, 1])
        warm = sb("warm", [128, 1])
        zero = sb("zero", [128, 1])
        one = sb("one", [128, 1])
        inside = sb("inside", [128, 1])
        late = sb("late", [128, 1])
        flag = sb("flag", [1, 2], I32)
        flag_f = sb("flag_f", [1, 1])
        kv = sb("kv", [128, 1])
        W_pair = sb("W_pair", [128, 128])
        W_edge = sb("W_edge", [D + 1, D])
        W_h = sb("W_h", [D + 1, D])
        W_mean = sb("W_mean", [D + 1, D + 1])
        W_out = sb("W_out", [D + 1, D])
        W2m = sb("W2m", [D, D])
        W2g = sb("W2g", [D, D])
        W2b_s = sb("W2b_s", [D, D])
        W1bT_s = sb("W1bT_s", [D, D])
        b1b_s = sb("b1b_s", [D, 1])
        L_mean = sb("L_mean", [D, D + 1])
        L_u0 = sb("L_u0", [D, D + 1])
        L_one = sb("L_one", [D, D + 1])
        rs = sb("rs", [D, 1])
        hx = sb("hx", [M, 2, 2, D])
        nhT = sb("nhT", [D + 1, M])
        tot = sb("tot", [D + 1, M])
        rc = sb("rc", [M, 2])
        y = sb("y", [M, D])
        y_exp = sb("y_exp", [M, D])
        nvT = sb("nvT", [D + 1, M])
        o_st = sb("o_st", [M, 2, D])
        hot_wide = ea[1][:, 0:WIDE]
        in_mask = x_sb[:, 0:TILES]
        late_mask = x_sb[:, TILES:TILES + GROUPS]

        ps = ctx.enter_context(nc.psum_tensor("ps", [128, 8, BANK], F32))
        def z_ps(par):
            return ps[:, par, 0:GT * D]

        def relu_ps(par):
            return ps[:, 6 + par, 0:GT * D]

        def agg_ps(par):
            return ps[0:D + 1, 2 + par, 0:WIN]
        u_ps = ps[0:D + 1, 7, 0:D]
        wm_ps = ps[0:D + 1, 7, D:2 * D]
        wo_ps = ps[0:D + 1, 7, 2 * D:3 * D]
        in_ps = ps[0:1, 5, 0:1]

        x_in = [sem(f"x_in{k}") for k in range(LCHUNKS)]
        w_first = sem("w_first")
        w_in = sem("w_in")
        dst_in = sem("dst_in")
        base_in = sem("base_in")
        iota_ok = sem("iota_ok")
        due_ok = sem("due_ok")
        ident_ok = sem("ident_ok")
        clear_ok = sem("clear_ok")
        ones_ok = sem("ones_ok")
        acc_clear = sem("acc_clear")
        dve_self = sem("dve_self")
        loop_self = sem("loop_self")
        slow_self = sem("slow_self")
        again_self = sem("again_self")
        xc_ok = sem("xc_ok")
        sq_ok = sem("sq_ok")
        var_ok = sem("var_ok")
        std_ok = sem("std_ok")
        h_ok = sem("h_ok")
        hT_ps_ok = sem("hT_ps_ok")
        hT_ok = sem("hT_ok")
        p_ps_ok = sem("p_ps_ok")
        p_copied = sem("p_copied")
        p_out = [sem(f"p_out{b}") for b in range(2)]
        h_out = sem("h_out")
        wprep_ok = sem("wprep_ok")
        small_ok = sem("small_ok")
        mask_ok = sem("mask_ok")
        flag_ok = sem("flag_ok")
        ea_in = [sem(f"ea_in{b}") for b in range(2)]
        idx_in = [sem(f"idx_in{b}") for b in range(2)]
        raw_in = [sem(f"raw_in{b}") for b in range(len(RAW_TILES))]
        g_in = [sem(f"g_in{s}") for s in range(RING)]
        slot_taken = sem("slot_taken")
        z_ok = sem("z_ok")
        zg_ok = sem("zg_ok")
        er_ok = sem("er_ok")
        s_ok = sem("s_ok")
        hot_ok = sem("hot_ok")
        agg_ok = sem("agg_ok")
        acc_ok = sem("acc_ok")
        slow_step = sem("slow_step")
        slow_tile = sem("slow_tile")
        slow_ea = sem("slow_ea")
        slow_idx = sem("slow_idx")
        slow_g = sem("slow_g")
        slow_z = sem("slow_z")
        slow_zg = sem("slow_zg")
        slow_er = sem("slow_er")
        slow_s = sem("slow_s")
        slow_hot = sem("slow_hot")
        slow_agg = sem("slow_agg")
        slow_acc = sem("slow_acc")

        class NodeSems:
            def __init__(self, pre):
                self.hT_ps = sem(pre + "hT_ps")
                self.hT = sem(pre + "hT")
                self.tot = sem(pre + "tot")
                self.yz = sem(pre + "yz")
                self.y1 = sem(pre + "y1")
                self.er = sem(pre + "er")
                self.v = sem(pre + "v")
                self.vT_ps = sem(pre + "vT_ps")
                self.vT = sem(pre + "vT")
                self.o_ps = sem(pre + "o_ps")
                self.o = sem(pre + "o")

        nd = NodeSems("node_")
        ag = NodeSems("again_")
        node_step = sem("node_step")
        hx_in = [sem(f"hx_in{b}") for b in range(2)]
        o_out = [sem(f"o_out{b}") for b in range(2)]
        again_go = sem("again_go")
        again_hx = sem("again_hx")
        again_out = sem("again_out")

        x_v = x.rearrange("(p t) d -> p (t d)", t=NT)
        P_v = P_dram.rearrange("(p t) d -> p (t d)", t=NT)
        h_v = h_dram.rearrange("(p t) d -> p (t d)", t=NT)
        N_W = 11 * 16
        PARTS = ((0, SPLIT), (SPLIT, NP))

        ln_cols = [slice(sum(LN_TILES[:k]) * D, sum(LN_TILES[:k + 1]) * D) for k in range(LCHUNKS)]
        ln_chunks = [(NP, x_sb[0:NP, cols].rearrange("p (t d) -> p t d", d=D), n, False)
                     for cols, n in zip(ln_cols, LN_TILES)]
        raw_first = [sum(RAW_TILES[:j]) for j in range(len(RAW_TILES) + 1)]
        ln_chunks += [(128, raw[:, t:t + n, :], n, True) for t, n in zip(raw_first, RAW_TILES)]
        units, first_unit = [], []
        for k, (_, _, n, _) in enumerate(ln_chunks):
            first_unit.append(len(units))
            units += [(k, t, min(QT, n - t)) for t in range(0, n, QT)]
        first_unit.append(len(units))
        CLEARS = 6

        def load_x(eng, chunks):
            for k in chunks:
                for a, b in PARTS:
                    eng.dma_start(x_sb[a:b, ln_cols[k]], x_v[a:b, ln_cols[k]]).then_inc(x_in[k], 16)

        block = ctx.enter_context(nc.Block())

        @block.sync
        def _(sp):
            def load_idx(c, par):
                sp.dma_start(idx[par][:, :], src_t[:, bass.ds(c * CHUNK_TILES, CHUNK_TILES)]).then_inc(idx_in[par], 16)

            def load_edges(c, par):
                sp.dma_start(ea[par][0:D, :], edge_t[bass.ds(c, 1), :, :].rearrange("c d e -> (c d) e")
                             ).then_inc(ea_in[par], 16)

            def load_nodes(m, par, signal):
                for j, t in enumerate((h_dram, x)):
                    sp.dma_start(hx[:, par, j, :], t[bass.ds(m * M, M), :]).then_inc(signal, 16)

            for c in range(RAW):
                load_idx(c, c)
            load_x(sp, range(2, LCHUNKS))
            sp.wait_ge(clear_ok, 1)
            for j in range(2):
                sp.dma_start(W_pair[j * D:(j + 1) * D, j * D:(j + 1) * D], W1a[0:D, :]).then_inc(w_first, 16)
            for dst_ap, src_ap in (
                (W_h[0:D, :], W2a[0:D, :]), (W_h[D:D + 1, :], b2a),
                (L_u0[:, D:D + 1], u0), (W2g[:, :], W2a[2 * D:3 * D, :]), (W_edge[0:D, :], W1a[D:2 * D, :]), (W_edge[D:D + 1, :], b1a),
                (W2m[:, :], W2a[D:2 * D, :]), (W1bT_s[:, :], W1bT), (b1b_s[:, :], b1b), (W2b_s[:, :], W2b),
                (W_out[D:D + 1, :], b2b),
            ):
                sp.dma_start(dst_ap, src_ap).then_inc(w_in, 16)
            sp.dma_start(base_i[:, :], dst_first.broadcast_to((128, GROUPS))).then_inc(base_in, 16)
            sp.dma_start(dstl[:, :].bitcast(I32), dst_t).then_inc(dst_in, 16)
            load_edges(0, 0)
            load_edges(1, 1)
            for k in range(LCHUNKS):
                cols = ln_cols[k]
                sp.wait_ge(h_ok, k + 1)
                for a, b in PARTS:
                    sp.dma_start(h_v[a:b, cols], x_sb[a:b, cols]).then_inc(h_out, 16)
                sp.wait_ge(p_copied, first_unit[k + 1])
                for a, b in PARTS:
                    sp.dma_start(P_v[a:b, cols], P_st[a:b, k % 2, 0:LN_TILES[k], :].rearrange("p t d -> p (t d)")
                                 ).then_inc(p_out[k % 2], 16)

            def step(c, par, n, waits=True, next_idx=True):
                if next_idx:
                    if waits:
                        sp.wait_ge(g_in[(1 - par) * CG + CG - 1], n * (16 * GT))
                    load_idx(c + 1, 1 - par)
                sp.wait_ge(z_ok, (c - 1) * CG)
                load_edges(c, par)
                if waits:
                    sp.wait_ge(nd.o, c - 3)
                load_nodes(c - 2, par, hx_in[par])

            for j in range(len(RAW_TILES)):
                sp.wait_ge(raw_in[j], 16 * RAW_TILES[j])
                if raw_first[j] < CHUNK_TILES <= raw_first[j + 1]:
                    load_idx(2, 0)
            load_idx(3, 1)
            sp.wait_ge(h_out, LCHUNKS * 32)
            step(2, 0, 0, waits=False, next_idx=False)
            sp.wait_ge(g_in[CG - 1], 16 * GT)
            load_idx(4, 0)
            step(3, 1, 0, waits=False, next_idx=False)
            with sp.Fori(0, (CHUNKS - 5) // 2) as i:
                step(i * 2 + 4, 0, i + 1)
                step(i * 2 + 5, 1, i + 2)
            step(CHUNKS - 1, 0, 0, next_idx=False)
            for m in (CHUNKS - 2, CHUNKS - 1):
                sp.wait_ge(nd.o, m - 1)
                load_nodes(m, m % 2, hx_in[m % 2])

            sp.wait_ge(flag_ok, 1)
            with sp.If(sp.value_load(flag[0:1, 0:1], min_val=0, max_val=2 * EDGES) != 0):
                with sp.Fori(0, CHUNKS) as c:
                    with sp.Fori(0, CHUNK_TILES) as k:
                        t = c * CHUNK_TILES + k
                        sp.wait_ge(slow_tile, t + 1)
                        sp.sem_inc(slow_step, 1)
                        sp.dma_start(idx[0][:, 0:1], src_t[:, bass.ds(t, 1)], allow_slow_non_contiguous=True
                                     ).then_inc(slow_idx, 16)
                        sp.dma_start(ea[0][0:D, 0:TILE],
                                     edge_t[bass.ds(c, 1), :, bass.ds(k * TILE, TILE)].rearrange("c d e -> (c d) e")
                                     ).then_inc(slow_ea, 16)
            with sp.If(sp.value_load(flag[0:1, 1:2], min_val=0, max_val=2 * EDGES) != 0):
                with sp.Fori(0, CHUNKS) as m:
                    sp.wait_ge(again_go, m + 1)
                    load_nodes(m, 0, again_hx)

        @block.gpsimd
        def _(pool):
            def gather(dst_rows, table, par, tile, signal):
                pool.indirect_dma_start(dst_rows, None, table,
                                        bass.IndirectOffsetOnAxis(idx[par][:, tile:tile + 1], 0)).then_inc(signal, 16)

            nc.gpsimd.memset(ident[:, :], 0.0).then_inc(ident_ok, 1)
            pool.wait_ge(ident_ok, 1)
            nc.gpsimd.affine_select(out=ident[:, :], in_=ident[:, :], compare_op=ALU.not_equal, fill=1.0, base=0,
                                    pattern=[[-1, 128]], channel_multiplier=1).then_inc(ident_ok, 1)
            for c in range(RAW):
                pool.wait_ge(idx_in[c], 16)
                for t in range(CHUNK_TILES):
                    j = max(j for j in range(len(RAW_TILES)) if raw_first[j] <= c * CHUNK_TILES + t)
                    gather(raw[:, c * CHUNK_TILES + t, :], x, c, t, raw_in[j])
                if c == 0:
                    nc.gpsimd.iota(iota_i[:, :], [[1, WIDE]], base=0, channel_multiplier=0).then_inc(iota_ok, 1)
            pool.wait_ge(p_out[0], 32 * ((LCHUNKS + 1) // 2))
            pool.wait_ge(p_out[1], 32 * (LCHUNKS // 2))

            def gather_chunk(c, par, loads, first=False):
                pool.wait_ge(idx_in[par], loads * 16)
                pool.sem_inc(slot_taken, 1)
                for q in range(CG):
                    if not first:
                        pool.wait_ge(zg_ok, c * CG + (q + 1 - RING))
                        pool.sem_inc(slot_taken, 1)
                    s = par * CG + q
                    for t in range(GT):
                        gather(G[:, s, t * D:(t + 1) * D], P_dram, par, q * GT + t, g_in[s])

            gather_chunk(2, 0, 2, first=True)
            gather_chunk(3, 1, 2, first=True)
            nc.gpsimd.iota(due_i[:, :], [[M, CHUNKS], [0, CG]], base=-M, channel_multiplier=0).then_inc(due_ok, 1)
            with pool.Fori(0, (CHUNKS - 5) // 2) as i:
                gather_chunk(i * 2 + 4, 0, i + 3)
                gather_chunk(i * 2 + 5, 1, i + 3)
            gather_chunk(CHUNKS - 1, 0, (CHUNKS + 1) // 2)

            pool.wait_ge(flag_ok, 1)
            with pool.If(pool.value_load(flag[0:1, 0:1], min_val=0, max_val=2 * EDGES) != 0):
                with pool.Fori(0, TILES) as t:
                    pool.wait_ge(slow_tile, t + 1)
                    pool.wait_ge(slow_idx, (t + 1) * 16)
                    pool.sem_inc(slow_step, 1)
                    gather(G[:, 0, 0:D], P_dram, 0, 0, slow_g)

        @block.scalar
        def _(act):
            act.sem_inc(o_out[0], 16)
            act.sem_inc(o_out[1], 16)
            act.sem_inc(again_out, 16)
            load_x(act, range(0, 2))
            act.wait_ge(clear_ok, 1)
            nc.scalar.activation(warm[:, :], eps[:, :], ACT.Sqrt)

            def square(k):
                rows, tiles, n, _ = ln_chunks[k]
                act.wait_ge(xc_ok, k + 1)
                if k >= 2:
                    act.wait_ge(var_ok, k - 1)
                nc.scalar.activation(sq[0:rows, k % 2, 0:n, :], tiles, ACT.Square).then_inc(sq_ok, 1)

            def deviation(k):
                rows, _, n, _ = ln_chunks[k]
                act.wait_ge(var_ok, k + 1)
                nc.scalar.activation(stat[0:rows, k % 2, 2, 0:n], stat[0:rows, k % 2, 1, 0:n], ACT.Sqrt, bias=eps[0:rows, :],
                                     scale=1.0 / D).then_inc(std_ok, 1)

            def copy_hT(n):
                k, _, nt = units[n]
                act.wait_ge(hT_ps_ok, n + 1)
                if n >= 2:
                    act.wait_ge(p_ps_ok, n - 1)
                used = nt // 2 * ln_chunks[k][0]
                nc.scalar.copy(hT[:, n % 2, 0:used], ps[:, n % 2, 0:used]).then_inc(hT_ok, 1)

            def copy_p(n):
                k, t0, nt = units[n]
                rows, tiles, _, gathered = ln_chunks[k]
                to = tiles if gathered else P_st[:, k % 2, :, :]
                if not gathered and k >= 2 and t0 == 0:
                    act.wait_ge(p_out[k % 2], 32 * (k // 2))
                act.wait_ge(p_ps_ok, n + 1)
                nc.scalar.copy(to[:, t0:t0 + nt, :], ps[0:rows, 2 + n % 2, 0:nt * D].rearrange("p (t d) -> p t d", d=D)
                               ).then_inc(p_copied, 1)

            cleared = 0

            def clear_part():
                nonlocal cleared
                end = ACC_COLS if cleared == CLEARS - 1 else (cleared + 1) * (ACC_COLS // CLEARS)
                start = cleared * (ACC_COLS // CLEARS)
                nc.scalar.copy(acc[:, start:end], zero[:, :].broadcast_to((128, end - start))).then_inc(acc_clear, 1)
                cleared += 1

            clear_part()
            square(0)
            clear_part()
            deviation(0)
            square(1)
            last_ln = len(ln_chunks) - 1
            for k in range(last_ln + 1):
                if k == last_ln:
                    clear_part()
                    clear_part()
                    square(k)
                    deviation(k)
                for j, n in enumerate(range(first_unit[k], first_unit[k + 1])):
                    copy_hT(n)
                    if j > 0 or 0 < k < LCHUNKS:
                        copy_p(n - 1)
                    if j == 0 and k + 1 < last_ln:
                        deviation(k + 1)
                    if j == 2:
                        if k + 2 < last_ln and k != LCHUNKS - 1:
                            square(k + 2)
                        if k in (1, LCHUNKS):
                            clear_part()
                if k >= LCHUNKS - 1:
                    copy_p(first_unit[k + 1] - 1)
                if k == LCHUNKS - 1 and k + 2 < last_ln:
                    square(k + 2)
            assert cleared == CLEARS

            def exp_relu(c, par, q, first=False):
                slot = (par + q) % 2
                act.wait_ge(zg_ok, c * CG + (q + 1))
                if not (first and q < 2):
                    act.wait_ge(s_ok, c * CG + (q - 1))
                nc.scalar.activation(E[:, slot, :], Z[:, slot, :], ACT.Exp, bias=ln_alpha[:, :])
                nc.scalar.activation(relu_ps(slot), Z[:, slot, :], ACT.Relu).then_inc(er_ok, 1)

            def node_hT(m, w):
                act.wait_ge(w.hT_ps, m + 1)
                nc.scalar.copy(nhT[0:D, :], ps[0:D, 4, 0:M]).then_inc(w.hT, 1)

            def node_exp(m, w):
                act.wait_ge(w.y1, m + 1)
                nc.scalar.activation(y_exp[:, :], y[:, :], ACT.Exp, bias=ln_alpha[0:M, :])
                nc.scalar.activation(y[:, :], y[:, :], ACT.Relu).then_inc(w.er, 1)

            def node_vT(m, w):
                act.wait_ge(w.vT_ps, m + 1)
                nc.scalar.copy(nvT[0:D, :], ps[0:D, 4, 0:M]).then_inc(w.vT, 1)

            def node_store(m, par, w, signal):
                act.wait_ge(w.o, m + 1)
                act.dma_start(out[bass.ds(m * M, M), :], o_st[:, par, :]).then_inc(signal, 16)

            def chunk(c, par):
                m = c - 2
                exp_relu(c, par, 0)
                node_hT(m, nd)
                exp_relu(c, par, 1)
                exp_relu(c, par, 2)
                node_exp(m, nd)
                exp_relu(c, par, 3)
                node_vT(m, nd)
                exp_relu(c, par, 4)
                node_store(m, par, nd, o_out[par])

            for c in range(RAW):
                for q in range(CG):
                    exp_relu(c, c, q, first=c == 0)
            with act.Fori(0, (CHUNKS - 3) // 2) as i:
                chunk(i * 2 + 2, 0)
                chunk(i * 2 + 3, 1)
            chunk(CHUNKS - 1, 0)
            node_hT(CHUNKS - 2, nd)

            act.wait_ge(flag_ok, 1)
            with act.If(act.value_load(flag[0:1, 0:1], min_val=0, max_val=2 * EDGES) != 0):
                with act.Fori(0, TILES) as t:
                    act.wait_ge(slow_zg, t + 1)
                    nc.scalar.activation(E[:, 0, 0:D], Z[:, 0, 0:D], ACT.Exp, bias=ln_alpha[:, :])
                    nc.scalar.activation(ps[:, 6, 0:D], Z[:, 0, 0:D], ACT.Relu).then_inc(slow_er, 1)

            def node_tile(m, par, w, signal, early=False):
                if not early:
                    node_hT(m, w)
                node_exp(m, w)
                node_vT(m, w)
                node_store(m, par, w, signal)

            for m in (CHUNKS - 2, CHUNKS - 1):
                node_tile(m, m % 2, nd, o_out[m % 2], early=m == CHUNKS - 2)
            for b in range(2):
                act.wait_ge(o_out[b], 16 + 16 * ((CHUNKS + 1 - b) // 2))
            with act.If(act.value_load(flag[0:1, 1:2], min_val=0, max_val=2 * EDGES) != 0):
                with act.Fori(0, CHUNKS) as m:
                    node_tile(m, 0, ag, again_out)
                act.wait_ge(again_out, 16 + 16 * CHUNKS)

        @block.vector
        def _(dve):
            HALF = (CHUNKS - 3) // 4
            steps = {dve_self: 0, slow_self: 0}

            def link(ins, s=dve_self):
                steps[s] += 1
                ins.then_inc(s, 1)
                dve.wait_ge(s, steps[s])

            def over_tiles(col, rows, n):
                return col.rearrange("p (t o) -> p t o", o=1).broadcast_to((rows, n, D))

            nc.vector.memset(W_pair[:, :], 0.0)
            nc.vector.memset(L_u0[:, :], 0.0)
            nc.vector.memset(L_one[:, :], 0.0)
            nc.vector.memset(W_mean[:, :], 0.0)
            nc.vector.memset(ln_alpha[:, :], float(np.log(ALPHA)))
            nc.vector.memset(eps[:, :], EPS)
            nc.vector.memset(zero[:, :], 0.0)
            nc.vector.memset(one[:, :], 1.0)
            nc.vector.memset(nhT[D:D + 1, :], 1.0)
            nc.vector.memset(nvT[D:D + 1, :], 1.0)
            link(nc.vector.memset(S[:, :, :, D:D + 1], 1.0))
            nc.vector.memset(L_one[:, D:D + 1], 1.0)
            nc.vector.memset(W_mean[D:D + 1, D:D + 1], 1.0).then_inc(clear_ok, 1)

            def centre(k):
                rows, h, n, gathered = ln_chunks[k]
                if gathered:
                    dve.wait_ge(raw_in[k - LCHUNKS], 16 * n)
                else:
                    dve.wait_ge(x_in[k], 32)
                st = stat[0:rows, k % 2, :, 0:n]
                link(nc.vector.tensor_reduce(out=st[:, 0, :], in_=h, op=ALU.add, axis=AX.X))
                link(nc.vector.tensor_scalar(st[:, 3, :], st[:, 0, :], -1.0 / D, None, ALU.mult))
                nc.vector.tensor_tensor(h, h, over_tiles(st[:, 3, :], rows, n), ALU.add).then_inc(xc_ok, 1)

            def variance(k):
                rows, _, n, _ = ln_chunks[k]
                dve.wait_ge(sq_ok, k + 1)
                nc.vector.tensor_reduce(out=stat[0:rows, k % 2, 1, 0:n], in_=sq[0:rows, k % 2, 0:n, :], op=ALU.add,
                                        axis=AX.X).then_inc(var_ok, 1)

            def normalise(k):
                rows, h, n, _ = ln_chunks[k]
                st = stat[0:rows, k % 2, :, 0:n]
                dve.wait_ge(std_ok, k + 1)
                link(nc.vector.reciprocal(st[:, 3, :], st[:, 2, :]))
                nc.vector.scalar_tensor_tensor(out=h, in0=h, scalar=0.0, in1=over_tiles(st[:, 3, :], rows, n),
                                               op0=ALU.max, op1=ALU.mult).then_inc(h_ok, 1)

            def ones_row(b):
                nc.vector.memset(ea[b][D:D + 1, :], 1.0).then_inc(ones_ok, 1)

            def prepare_weights():
                link(nc.vector.tensor_reduce(out=rs[:, 0:1], in_=W1bT_s[:, :], op=ALU.add, axis=AX.X))
                nc.vector.scalar_tensor_tensor(out=L_mean[:, D:D + 1], in0=rs[:, 0:1], scalar=-ALPHA * LAM,
                                               in1=b1b_s[:, :], op0=ALU.mult, op1=ALU.add)
                nc.vector.tensor_scalar(L_mean[:, 0:D], W1bT_s[:, :], LAM, None, ALU.mult)
                nc.vector.tensor_scalar(W_out[0:D, :], W2b_s[:, :], LAM, None, ALU.mult).then_inc(wprep_ok, 1)

            def finish_weights():
                dve.wait_ge(small_ok, 3)
                nc.vector.tensor_copy(W_mean[:, 0:D], wm_ps)
                nc.vector.scalar_tensor_tensor(out=W_out[D:D + 1, :], in0=wo_ps[D:D + 1, :], scalar=-ALPHA * LAM,
                                               in1=W_out[D:D + 1, :], op0=ALU.mult, op1=ALU.add)
                nc.vector.tensor_tensor(W_h[D:D + 1, :], W_h[D:D + 1, :], u_ps[D:D + 1, :], ALU.add).then_inc(wprep_ok, 1)

            last = len(ln_chunks) - 1
            centre(0)
            centre(1)
            variance(0)
            normalise(0)
            for k in range(1, last):
                variance(k)
                if k == LCHUNKS:
                    ones_row(0)
                if k + 1 < last:
                    centre(k + 1)
                normalise(k)
            dve.wait_ge(w_in, N_W)
            prepare_weights()
            dve.wait_ge(base_in, 16)
            dve.wait_ge(dst_in, 16)
            nc.vector.tensor_tensor(
                dstl[:, :].rearrange("p (g t) -> p g t", t=GT),
                dstl[:, :].bitcast(I32).rearrange("p (g t) -> p g t", t=GT),
                base_i[:, :].rearrange("p (g o) -> p g o", o=1).broadcast_to((128, GROUPS, GT)), ALU.subtract)
            dve.wait_ge(iota_ok, 1)
            nc.vector.tensor_copy(iota[:, :], iota_i[:, :])
            finish_weights()
            centre(last)
            variance(last)
            normalise(last)
            ones_row(1)
            dve.wait_ge(acc_clear, CLEARS)

            def add_window(g, par):
                base = dve.value_load(base_i[0:1, bass.ds(g, 1)], min_val=0, max_val=NODES - 1)
                dve.wait_ge(agg_ok, g + 1)
                window = acc[0:D + 1, bass.ds(base, WIN)]
                nc.vector.tensor_tensor(window, window, agg_ps(par), ALU.add).then_inc(acc_ok, 1)

            def combine(c, par, q, first=False):
                rows = raw[:, c * CHUNK_TILES + q * GT:c * CHUNK_TILES + (q + 1) * GT, :].rearrange("p t d -> p (t d)") \
                    if isinstance(c, int) and c < RAW else G[:, par * CG + q, :]
                slot = (par + q) % 2
                if not first:
                    dve.wait_ge(agg_ok, c * CG + (q + 1 - CG))
                nc.vector.tensor_tensor(
                    hot[:, q, :, :], iota[:, 0:WIN].rearrange("p (o w) -> p o w", o=1).broadcast_to((128, GT, WIN)),
                    dstl[:, bass.ds(c * CHUNK_TILES + q * GT, GT)].rearrange("p (t o) -> p t o", o=1).broadcast_to(
                        (128, GT, WIN)), ALU.is_equal).then_inc(hot_ok, 1)
                if not (isinstance(c, int) and c < RAW):
                    dve.wait_ge(g_in[par * CG + q], gathers(c, par) * (16 * GT))
                dve.wait_ge(z_ok, c * CG + (q + 1))
                nc.vector.tensor_tensor(Z[:, slot, :], rows, z_ps(slot), ALU.add).then_inc(zg_ok, 1)
                dve.wait_ge(er_ok, c * CG + (q + 1))
                nc.vector.scalar_tensor_tensor(
                    out=S[:, q, :, 0:D], in0=E[:, slot, :].rearrange("p (t d) -> p t d", d=D), scalar=ALPHA,
                    in1=relu_ps(slot).rearrange("p (t d) -> p t d", d=D), op0=ALU.min, op1=ALU.add).then_inc(s_ok, 1)
                if not (first and q == 0):
                    if not (first and q == 1):
                        dve.wait_ge(acc_ok, c * CG + (q - 1))
                    add_window(c * CG + (q - 1), (par + q + 1) % 2)

            turn = [None]

            def gathers(c, par):
                return (CHUNKS - 1) // 2 if isinstance(c, int) else turn[0] + 1

            def node_totals(m, w):
                nc.vector.tensor_copy(tot[:, :], acc[0:D + 1, bass.ds(m * M, M)]).then_inc(w.tot, 1)

            def node_first(m, w, own):
                dve.wait_ge(w.yz, m + 1)
                nc.vector.tensor_scalar(rc[:, 0:1], ps[0:M, 5, 2 * D:2 * D + 1], 1.0, None, ALU.max).then_inc(own, 1)
                dve.wait_ge(own, m * 3 + 1)
                nc.vector.reciprocal(rc[:, 1:2], rc[:, 0:1]).then_inc(own, 1)
                dve.wait_ge(own, m * 3 + 2)
                nc.vector.tensor_scalar(y[:, :], ps[0:M, 5, D:2 * D], rc[:, 1:2], None, ALU.mult).then_inc(own, 1)
                dve.wait_ge(own, m * 3 + 3)
                nc.vector.tensor_tensor(y[:, :], y[:, :], ps[0:M, 5, 0:D], ALU.add).then_inc(w.y1, 1)

            def node_s(m, w):
                dve.wait_ge(w.er, m + 1)
                nc.vector.scalar_tensor_tensor(out=y[:, :], in0=y_exp[:, :], scalar=ALPHA, in1=y[:, :],
                                               op0=ALU.min, op1=ALU.add).then_inc(w.v, 1)

            def node_out(m, par, w, out_sem, stores):
                dve.wait_ge(out_sem, (stores + 1) * 16)
                dve.wait_ge(w.o_ps, m + 1)
                nc.vector.tensor_tensor(o_st[:, par, :], ps[0:M, 5, 0:D], hx[:, par, 1, :], ALU.add).then_inc(w.o, 1)

            def chunk(c, par, stores):
                m = c - 2
                combine(c, par, 0)
                dve.wait_ge(acc_ok, c * CG)
                node_totals(m, nd)
                combine(c, par, 1)
                node_first(m, nd, loop_self)
                combine(c, par, 2)
                node_s(m, nd)
                combine(c, par, 3)
                combine(c, par, 4)
                dve.wait_ge(hx_in[par], (stores + 1) * 32)
                node_out(m, par, nd, o_out[par], stores)

            for c in range(RAW):
                for q in range(CG):
                    combine(c, c, q, first=c == 0)

            def loop(a, b):
                with dve.Fori(a, b) as i:
                    turn[0] = i
                    chunk(i * 2 + 2, 0, i)
                    chunk(i * 2 + 3, 1, i)

            loop(0, HALF)
            dve.wait_ge(due_ok, 1)
            nc.vector.tensor_tensor(late_mask, base_i[:, :], due_i[:, :], ALU.is_lt)
            link(nc.vector.tensor_scalar(in_mask, dstl[:, :], 0.0, None, ALU.is_ge))
            nc.vector.tensor_reduce(out=late[:, :], in_=late_mask, op=ALU.add, axis=AX.X)
            link(nc.vector.scalar_tensor_tensor(out=in_mask, in0=dstl[:, :], scalar=float(WIN), in1=in_mask,
                                                op0=ALU.is_lt, op1=ALU.mult))
            nc.vector.tensor_reduce(out=inside[:, :], in_=in_mask, op=ALU.add, axis=AX.X).then_inc(mask_ok, 1)
            loop(HALF, (CHUNKS - 3) // 2)
            dve.wait_ge(small_ok, 4)
            link(nc.vector.tensor_scalar(flag_f[:, :], in_ps, -1.0, float(EDGES), ALU.mult, ALU.add))
            nc.vector.tensor_copy(flag[:, 0:1], flag_f[:, :])
            nc.vector.tensor_tensor(flag[:, 1:2], flag_f[:, :], late[0:1, :], ALU.add).then_inc(flag_ok, 1)
            chunk(CHUNKS - 1, 0, (CHUNKS - 3) // 2)
            dve.wait_ge(acc_ok, GROUPS - 1)
            add_window(GROUPS - 1, (GROUPS - 1) % 2)
            dve.wait_ge(acc_ok, GROUPS)

            with dve.If(dve.value_load(flag[0:1, 0:1], min_val=0, max_val=2 * EDGES) != 0):
                base_b = base_i[:, :].rearrange("p (g o) -> p g o", o=1).broadcast_to((128, GROUPS, GT))
                as_groups = lambda a: a.rearrange("p (g t) -> p g t", t=GT)
                link(nc.vector.tensor_tensor(as_groups(dstl[:, :]), as_groups(dstl[:, :]), base_b, ALU.add), slow_self)
                nc.vector.scalar_tensor_tensor(out=dstl[:, :], in0=in_mask, scalar=-2.0 * ACC_COLS, in1=dstl[:, :],
                                               op0=ALU.mult, op1=ALU.add).then_inc(slow_tile, 1)
                dve.wait_ge(slow_tile, 1)
                nc.vector.tensor_copy(kv[:, :], dstl[:, 0:1]).then_inc(slow_acc, 1)
                with dve.Fori(0, TILES) as t:
                    dve.wait_ge(slow_g, (t + 1) * 16)
                    dve.wait_ge(slow_z, t + 1)
                    nc.vector.tensor_tensor(Z[:, 0, 0:D], G[:, 0, 0:D], ps[:, 0, 0:D], ALU.add).then_inc(slow_zg, 1)
                    dve.wait_ge(slow_er, t + 1)
                    nc.vector.scalar_tensor_tensor(out=S[:, 0, 0, 0:D], in0=E[:, 0, 0:D], scalar=ALPHA, in1=ps[:, 6, 0:D],
                                                   op0=ALU.min, op1=ALU.add).then_inc(slow_s, 1)
                    dve.wait_ge(slow_acc, t * WIDES + 1)
                    nc.vector.tensor_copy(kv[:, :], dstl[:, bass.ds(t, 1)]).then_inc(slow_s, 1)
                    dve.wait_ge(slow_s, (t + 1) * 2)
                    dve.sem_inc(slow_step, 1)
                    with dve.Fori(0, WIDES) as v:
                        n = t * WIDES + v
                        dve.wait_ge(slow_acc, n + 1)
                        nc.vector.tensor_scalar(hot_wide, iota[:, :], kv[:, 0:1], None, ALU.is_equal).then_inc(slow_hot, 1)
                        dve.wait_ge(slow_agg, n + 1)
                        nc.vector.tensor_scalar(kv[:, :], kv[:, :], -float(WIDE), None, ALU.add)
                        wide = acc[0:D + 1, bass.ds(v * WIDE, WIDE)]
                        nc.vector.tensor_tensor(wide, wide, ps[0:D + 1, 2, :], ALU.add).then_inc(slow_acc, 1)
                    dve.wait_ge(slow_acc, t * WIDES + (WIDES + 1))
                    dve.sem_inc(slow_tile, 1)

            for m in (CHUNKS - 2, CHUNKS - 1):
                node_totals(m, nd)
                node_first(m, nd, loop_self)
                node_s(m, nd)
                dve.wait_ge(hx_in[m % 2], (m // 2 + 1) * 32)
                node_out(m, m % 2, nd, o_out[m % 2], m // 2)

            with dve.If(dve.value_load(flag[0:1, 1:2], min_val=0, max_val=2 * EDGES) != 0):
                for b in range(2):
                    dve.wait_ge(o_out[b], 16 + 16 * ((CHUNKS + 1 - b) // 2))
                dve.sem_inc(again_go, 1)
                with dve.Fori(0, CHUNKS) as m:
                    node_totals(m, ag)
                    node_first(m, ag, again_self)
                    node_s(m, ag)
                    dve.wait_ge(again_hx, (m + 1) * 32)
                    node_out(m, 0, ag, again_out, m)
                    dve.wait_ge(ag.o, m + 1)
                    dve.sem_inc(again_go, 1)

        @block.tensor
        def _(pe):
            mm = nc.tensor.matmul
            pe.wait_ge(ident_ok, 2)
            pe.wait_ge(w_first, 32)

            def products(n):
                k, _, nt = units[n]
                rows = ln_chunks[k][0]
                pe.wait_ge(hT_ok, n + 1)
                if n >= 2:
                    pe.wait_ge(p_copied, n - 1)
                for p in range(nt // 2):
                    last = mm(ps[0:rows, 2 + n % 2, p * 2 * D:(p + 1) * 2 * D], hT[:, n % 2, p * rows:(p + 1) * rows],
                              W_pair[:, :], start=True, stop=True)
                last.then_inc(p_ps_ok, 1)

            for n, (k, t0, nt) in enumerate(units):
                rows, tiles, _, _ = ln_chunks[k]
                pe.wait_ge(h_ok, k + 1)
                if n >= 2:
                    pe.wait_ge(hT_ok, n - 1)
                for p in range(nt // 2):
                    pair = tiles[:, t0 + 2 * p:t0 + 2 * p + 2, :].rearrange("p t d -> p (t d)")
                    last = nc.tensor.transpose(ps[:, n % 2, p * rows:(p + 1) * rows], pair, ident[0:rows, 0:rows])
                last.then_inc(hT_ps_ok, 1)
                if n > first_unit[k] or 0 < k < LCHUNKS:
                    products(n - 1)
                if k >= LCHUNKS - 1 and n == first_unit[k + 1] - 1:
                    products(n)
                if n == first_unit[-2] - 1:
                    pe.wait_ge(wprep_ok, 1)
                    mm(u_ps, L_u0[:, :], W2g[:, :], start=True, stop=True).then_inc(small_ok, 1)
                    mm(wm_ps, L_mean[:, :], W2m[:, :], start=True, stop=True).then_inc(small_ok, 1)
                    mm(wo_ps, L_one[:, :], W2b_s[:, :], start=True, stop=True).then_inc(small_ok, 1)
            pe.wait_ge(wprep_ok, 2)
            pe.wait_ge(p_copied, len(units))

            def sum_group(c, par, q, first=False):
                pq = (q - 1) % CG
                pe.wait_ge(s_ok, c * CG + q)
                pe.wait_ge(hot_ok, c * CG + q)
                if not (first and q < 3):
                    pe.wait_ge(acc_ok, c * CG + (q - 2))
                for t in range(GT):
                    last = mm(agg_ps((par + q + 1) % 2), S[:, pq, t, :], hot[:, pq, t, :], start=(t == 0), stop=(t == GT - 1))
                last.then_inc(agg_ok, 1)

            def edge_group(c, par, loads, q, first=False):
                slot = (par + q) % 2
                if q == 0:
                    pe.wait_ge(ea_in[par], loads * 16)
                    if isinstance(c, int) and c < 2:
                        pe.wait_ge(ones_ok, c + 1)
                if not (first and q < 2):
                    pe.wait_ge(zg_ok, c * CG + (q - 1))
                for t in range(GT):
                    e0 = (q * GT + t) * TILE
                    last = mm(z_ps(slot)[:, t * D:(t + 1) * D], ea[par][0:D + 1, e0:e0 + TILE], W_edge[:, :],
                              start=True, stop=True)
                last.then_inc(z_ok, 1)
                if not (first and q == 0):
                    sum_group(c, par, q, first)

            def node_hT(m, par, w, hx_sem, loads):
                pe.wait_ge(hx_sem, loads * 32)
                pe.sem_inc(node_step, 1)
                nc.tensor.transpose(ps[0:D, 4, 0:M], hx[:, par, 0, :], ident[0:M, 0:M]).then_inc(w.hT_ps, 1)

            def node_first(m, w):
                pe.wait_ge(w.hT, m + 1)
                pe.wait_ge(w.tot, m + 1)
                mm(ps[0:M, 5, 0:D], nhT[:, :], W_h[:, :], start=True, stop=True)
                mm(ps[0:M, 5, D:2 * D + 1], tot[:, :], W_mean[:, :], start=True, stop=True).then_inc(w.yz, 1)

            def node_vT(m, w):
                pe.wait_ge(w.v, m + 1)
                pe.sem_inc(node_step, 1)
                nc.tensor.transpose(ps[0:D, 4, 0:M], y[:, :], ident[0:M, 0:M]).then_inc(w.vT_ps, 1)

            def node_out(m, w):
                pe.wait_ge(w.vT, m + 1)
                mm(ps[0:M, 5, 0:D], nvT[:, :], W_out[:, :], start=True, stop=True).then_inc(w.o_ps, 1)

            def chunk(c, par, loads):
                m = c - 2
                edge_group(c, par, loads, 0)
                node_hT(m, par, nd, hx_in[par], loads - 1)
                edge_group(c, par, loads, 1)
                node_first(m, nd)
                edge_group(c, par, loads, 2)
                edge_group(c, par, loads, 3)
                node_vT(m, nd)
                edge_group(c, par, loads, 4)
                node_out(m, nd)

            for c in range(RAW):
                for q in range(CG):
                    edge_group(c, c, 1, q, first=c == 0)
            with pe.Fori(0, (CHUNKS - 3) // 2) as i:
                chunk(i * 2 + 2, 0, i + 2)
                chunk(i * 2 + 3, 1, i + 2)
            pe.wait_ge(mask_ok, 1)
            pe.wait_ge(nd.o, CHUNKS - 3)
            mm(in_ps, inside[:, :], one[:, :], start=True, stop=True).then_inc(small_ok, 1)
            chunk(CHUNKS - 1, 0, (CHUNKS + 1) // 2)
            node_hT(CHUNKS - 2, 1, nd, hx_in[1], (CHUNKS - 1) // 2)
            sum_group(CHUNKS, CHUNKS % 2, 0)

            pe.wait_ge(flag_ok, 1)
            with pe.If(pe.value_load(flag[0:1, 0:1], min_val=0, max_val=2 * EDGES) != 0):
                with pe.Fori(0, TILES) as t:
                    pe.wait_ge(slow_ea, (t + 1) * 16)
                    mm(ps[:, 0, 0:D], ea[0][0:D + 1, 0:TILE], W_edge[:, :], start=True, stop=True).then_inc(slow_z, 1)
                    pe.wait_ge(slow_s, (t + 1) * 2)
                    pe.sem_inc(slow_step, 1)
                    with pe.Fori(0, WIDES) as v:
                        pe.wait_ge(slow_hot, t * WIDES + v + 1)
                        mm(ps[0:D + 1, 2, :], S[:, 0, 0, :], hot_wide, start=True, stop=True).then_inc(slow_agg, 1)

            def node_tile(m, par, w, hx_sem, loads, early=False):
                if not early:
                    node_hT(m, par, w, hx_sem, loads)
                node_first(m, w)
                node_vT(m, w)
                node_out(m, w)

            for m in (CHUNKS - 2, CHUNKS - 1):
                node_tile(m, m % 2, nd, hx_in[m % 2], m // 2 + 1, early=m == CHUNKS - 2)
            with pe.If(pe.value_load(flag[0:1, 1:2], min_val=0, max_val=2 * EDGES) != 0):
                with pe.Fori(0, CHUNKS) as m:
                    node_tile(m, 0, ag, again_hx, m + 1)


def kernel(x, src, dst, edge_attr_64, L0_gnn_u, L0_gnn_W1a, L0_gnn_b1a, L0_gnn_W1b, L0_gnn_b1b, L0_gnn_W2a, L0_gnn_b2a,
           L0_gnn_W2b, L0_gnn_b2b):
    import concourse.bacc as bacc
    from concourse.bass_utils import run_bass_kernel_spmd

    a = np.asarray
    arrays = {
        "x": a(x),
        "src_t": np.ascontiguousarray(a(src).reshape(TILES, TILE).T),
        "dst_t": np.ascontiguousarray(a(dst).reshape(TILES, TILE).T),
        "dst_first": np.ascontiguousarray(a(dst).reshape(GROUPS, GT * TILE)[:, 0].reshape(1, GROUPS)),
        "edge_t": np.ascontiguousarray(a(edge_attr_64).reshape(CHUNKS, CE, D).transpose(0, 2, 1)),
        "u0": np.ascontiguousarray(a(L0_gnn_u)[0].reshape(D, 1)),
        "W1a": a(L0_gnn_W1a),
        "b1a": a(L0_gnn_b1a).reshape(1, D),
        "W1bT": np.ascontiguousarray(a(L0_gnn_W1b).T),
        "b1b": a(L0_gnn_b1b).reshape(D, 1),
        "W2a": a(L0_gnn_W2a),
        "b2a": a(L0_gnn_b2a).reshape(1, D),
        "W2b": a(L0_gnn_W2b),
        "b2b": a(L0_gnn_b2b).reshape(1, D),
    }
    nc = bacc.Bacc("TRN2", target_bir_lowering=False, num_devices=1)
    args = [nc.dram_tensor(name, v.shape, mybir.dt.from_np(v.dtype), kind="ExternalInput").ap() for name, v in arrays.items()]
    out = nc.dram_tensor("out", (NODES, D), F32, kind="ExternalOutput").ap()
    build(nc, *args, out)
    r = run_bass_kernel_spmd(nc, [arrays], core_ids=[0])
    return r.results[0]["out"]
```
